# Optimizing a Trainium2 kernel written in Bass

```python
import numpy as np
import jax
import jax.numpy as jnp

def _softmax(x, axis=-1):
    return jax.nn.softmax(x, axis=axis)

def _gelu(x):
    return jax.nn.gelu(x, approximate=True)

def _silu(x):
    return jax.nn.silu(x)

def _sigmoid(x):
    return jax.nn.sigmoid(x)

def _layernorm(x, axis=-1, eps=1e-05):
    m = jnp.mean(x, axis=axis, keepdims=True)
    v = jnp.var(x, axis=axis, keepdims=True)
    return (x - m) / jnp.sqrt(v + eps)

def _scatter_add(tgt, idx, src, axis=0):
    return tgt.at[idx].add(src)

def _segment_sum(src, seg, n):
    return jax.ops.segment_sum(src, seg, n)
kernel_name = 'mk_gnn_preln_d2_gnn_r64_d9cd01'

def setup_inputs(seed: int=0):
    np.random.seed(seed)
    _w = jnp.asarray

    def _rec_inputs():
        import jax
        import jax.numpy as jnp
        _gk = jax.random.key(seed)
        x = -0.0003713 + 1 * jax.random.normal(jax.random.fold_in(_gk, 1), (100000, 128), jnp.float32)
        src = jax.random.randint(jax.random.fold_in(_gk, 2), (50000,), 0, 100000, jnp.int32)
        dst = jnp.minimum((100000 * jax.random.uniform(jax.random.fold_in(_gk, 3), (50000,)) ** 2.0).astype(jnp.int32), 99999)
        _o = jnp.argsort(dst, stable=True)
        src = src[_o]
        dst = dst[_o]
        edge_type_64 = jax.random.randint(jax.random.fold_in(_gk, 12), (50000,), 0, 64, jnp.int32)
        return (x, src, dst, edge_type_64)
    x, src, dst, edge_type_64 = _rec_inputs()

    def _L0_gnn_setup():
        import jax, jax.numpy as jnp
        import numpy as np
        K = 10
        ALPHA = 0.1
        N_NODES = 100000
        N_EDGES = 50000
        D_FEAT = 128
        key = jax.random.key(seed)
        k1, k2 = jax.random.split(key)
        x = jax.random.normal(k1, (N_NODES, D_FEAT), dtype=jnp.float32)
        edge_index = jax.random.randint(k2, (2, N_EDGES), 0, N_NODES, dtype=jnp.int64)
        return {'x': x, 'edge_index': edge_index, 'n_nodes': N_NODES}
    _L0_gnn_all = _L0_gnn_setup()
    _L0_gnn_in = {k: v for k, v in _L0_gnn_all.items() if k in ()}
    del _L0_gnn_all

    def _L1_gnn_setup():
        import jax, jax.numpy as jnp
        import numpy as np
        N_HOPS = 3
        N_ENTITIES = 100000
        EMB = 128
        N_EDGES = 9375
        N_REL = 64
        key = jax.random.key(seed)
        k1, k2, k3, k4, k5, k6 = jax.random.split(key, 6)
        entity_emb = jax.random.normal(k1, (N_ENTITIES, EMB), dtype=jnp.float32)
        edge_emb = jax.random.normal(k2, (N_REL, EMB), dtype=jnp.float32)
        q_w = jax.random.normal(k3, (EMB, EMB), dtype=jnp.float32) * (1.0 / np.sqrt(EMB))
        k_w = jax.random.normal(k4, (EMB, EMB), dtype=jnp.float32) * (1.0 / np.sqrt(EMB))
        edge_index = jax.random.randint(k5, (2, N_EDGES), 0, N_ENTITIES, dtype=jnp.int64)
        edge_type = jax.random.randint(k6, (N_EDGES,), 0, N_REL, dtype=jnp.int64)
        return {'entity_emb': entity_emb, 'edge_emb': edge_emb, 'q_w': q_w, 'k_w': k_w, 'edge_index': edge_index, 'edge_type': edge_type, 'mess_dropout': 0}
    _L1_gnn_all = _L1_gnn_setup()
    _L1_gnn_in = {k: v for k, v in _L1_gnn_all.items() if k in ('edge_emb', 'q_w', 'k_w')}
    del _L1_gnn_all
    return {'x': x, 'src': src, 'dst': dst, 'edge_type_64': edge_type_64, 'L1_gnn_edge_emb': _L1_gnn_in['edge_emb'], 'L1_gnn_q_w': _L1_gnn_in['q_w'], 'L1_gnn_k_w': _L1_gnn_in['k_w']}

def reference(x, src, dst, edge_type_64, L1_gnn_edge_emb, L1_gnn_q_w, L1_gnn_k_w):
    import jax
    import jax.numpy as jnp

    def _L0_gnn_ref(x, edge_index, n_nodes):
        import jax, jax.numpy as jnp
        import numpy as np
        K = 10
        ALPHA = 0.1
        N_NODES = 100000
        N_EDGES = 50000
        D_FEAT = 128
        row, col = (edge_index[0], edge_index[1])
        deg = jax.ops.segment_sum(jnp.ones(row.shape[0], dtype=x.dtype), row, num_segments=n_nodes)
        deg_inv_sqrt = jnp.where(deg > 0, jax.lax.rsqrt(deg), 0.0)
        norm = deg_inv_sqrt[row] * deg_inv_sqrt[col]

        def step(h, _):
            msg = jax.ops.segment_sum(norm[:, None] * h[col], row, num_segments=n_nodes)
            h_new = (1.0 - ALPHA) * msg + ALPHA * x
            return (h_new, None)
        h, _ = jax.lax.scan(step, x, None, length=K)
        return h

    def _L1_gnn_ref(entity_emb, edge_emb, q_w, k_w, edge_index, edge_type, mess_dropout):
        import jax, jax.numpy as jnp
        import numpy as np
        N_HOPS = 3
        N_ENTITIES = 100000
        EMB = 128
        N_EDGES = 9375
        N_REL = 64
        head = edge_index[0]
        tail = edge_index[1]
        rel = edge_emb[edge_type]
        n = entity_emb.shape[0]
        agg = entity_emb
        out = jnp.zeros_like(entity_emb)
        for _ in range(N_HOPS):
            h = agg[head]
            t = agg[tail]
            left = h @ q_w
            right = jnp.tanh(rel * t @ k_w)
            att = jnp.sum(left * right, axis=1)
            seg_max = jax.ops.segment_max(att, head, num_segments=n)
            e = jnp.exp(att - seg_max[head])
            seg_sum = jax.ops.segment_sum(e, head, num_segments=n)
            w = e / seg_sum[head]
            msg = w[:, None] * rel * t
            summed = jax.ops.segment_sum(msg, head, num_segments=n)
            cnt = jax.ops.segment_sum(jnp.ones_like(att), head, num_segments=n)
            agg = summed / jnp.maximum(cnt, 1.0)[:, None]
            norm = jnp.linalg.norm(agg, axis=1, keepdims=True)
            agg = agg / jnp.maximum(norm, 1e-12)
            out = out + agg + entity_emb
        return out
    edge_index = jnp.stack([src, dst])
    h = jnp.maximum(_layernorm(x, axis=-1), 0.0)
    x = x + _L0_gnn_ref(h, edge_index, 100000)
    h = jnp.maximum(_layernorm(x, axis=-1), 0.0)
    x = x + _L1_gnn_ref(h, L1_gnn_edge_emb, L1_gnn_q_w, L1_gnn_k_w, edge_index, edge_type_64, 0)
    return x

_drawn_inputs = setup_inputs


def setup_inputs(seed=0):
    import zlib

    import numpy as np

    out = dict(_drawn_inputs(seed))
    spreads = {}
    factors = {}
    for name, (base, spread) in spreads.items():
        noise = np.random.default_rng([zlib.crc32(name.encode()), seed]).standard_normal(out[name].shape)
        drawn = base * np.exp(spread * noise) if base else spread * noise
        out[name] = jnp.asarray(drawn.astype(out[name].dtype))
    for name, factor in factors.items():
        out[name] = (out[name] * factor).astype(out[name].dtype)
    return out
```

```python
import concourse.bass as bass
from concourse import mybir
from contextlib import ExitStack

F32 = mybir.dt.float32
BF16 = mybir.dt.bfloat16
F16 = mybir.dt.float16
I32 = mybir.dt.int32
ALU = mybir.AluOpType
ACT = mybir.ActivationFunctionType
AX = mybir.AxisListType
P = 128

NODES = 100000
EDGES = 50000
D = 128
RELATIONS = 64
TILES = 392
ROWS = TILES * P
LO = 256
HI = 391
TABLE = HI * LO
U = 7
STEPS = TILES // (2 * U)
REC = 4
BIG = 3.0e38


class Chain:

    def __init__(self, engine, sem, base=0):
        self.engine, self.sem, self.base, self.n = engine, sem, base, 0

    def link(self, instruction):
        self.n += 1
        instruction.then_inc(self.sem, 1)
        self.engine.wait_ge(self.sem, self.base + self.n)


class Phase(ExitStack):

    def __init__(self, nc):
        super().__init__()
        self.nc, self.used = nc, []

    def semaphore(self, name):
        handle = self.enter_context(self.nc.semaphore(name))
        self.used.append(handle.num)
        return handle

    def lasting(self, name):
        return self.nc.alloc_semaphore(name)

    def __exit__(self, *error):
        result = super().__exit__(*error)
        if error[0] is None:
            numbers = sorted(self.used)
            while numbers:
                run = [numbers.pop(0)]
                while numbers and numbers[0] == run[-1] + 1:
                    run.append(numbers.pop(0))
                self.nc.gpsimd.sem_clear(range(run[0], run[-1] + 1))
            self.nc.all_engine_barrier()
        return result


def constants(nc, c):
    with Phase(nc) as s:
        made = s.semaphore("const_made")
        block = s.enter_context(nc.Block())

        @block.gpsimd
        def _(pool):
            ch = Chain(pool, made)
            ch.link(pool.memset(c.ident[:], 0.0))
            ch.link(pool.affine_select(out=c.ident[:], in_=c.ident[:], compare_op=ALU.not_equal, fill=1.0,
                                       base=0, pattern=[[-1, P]], channel_multiplier=1))
            ch.link(pool.memset(c.ones[:], 1.0))
            ch.link(pool.affine_select(out=c.tri[:], in_=c.ones[:], compare_op=ALU.is_gt, fill=0.0,
                                       base=0, pattern=[[1, P]], channel_multiplier=-1))
            ch.link(pool.affine_select(out=c.rest16[:], in_=c.ones[:], compare_op=ALU.is_ge, fill=0.0,
                                       base=0, pattern=[[-1, P]], channel_multiplier=1))
            ch.link(pool.tensor_copy(c.tri16[:], c.tri[:]))
            ch.link(pool.memset(c.ones16[:], 1.0))
            ch.link(pool.affine_select(out=c.row_first[:], in_=c.ones[:], compare_op=ALU.is_equal, fill=0.0,
                                       base=0, pattern=[[0, P]], channel_multiplier=1))
            ch.link(pool.affine_select(out=c.row_last[:], in_=c.ones[:], compare_op=ALU.is_equal, fill=0.0,
                                       base=1 - P, pattern=[[0, P]], channel_multiplier=1))
            ch.link(pool.iota(c.count16[:], pattern=[[1, HI]], base=0, channel_multiplier=0,
                              allow_small_or_imprecise_dtypes=True))
            ch.link(pool.iota(c.part[:], pattern=[[1, 1]], base=0, channel_multiplier=1,
                              allow_small_or_imprecise_dtypes=True))


def split_digits(vec, ch, c):
    ch.link(vec.tensor_scalar(c.digit[:], c.rec[:, :, 0], LO - 1, None, ALU.bitwise_and))
    ch.link(vec.tensor_copy(c.lo[:], c.digit[:]))
    ch.link(vec.tensor_scalar(c.digit[:], c.rec[:, :, 0], 8, None, ALU.logical_shift_right))
    ch.link(vec.tensor_copy(c.hi[:], c.digit[:]))


def histogram(nc, c, src, dst, relation):
    with Phase(nc) as s:
        sem = lambda n: s.semaphore(n)
        loaded, packed, ready, counted, chain = sem("h_loaded"), sem("h_packed"), sem("h_ready"), sem("h_counted"), sem("h_chain")
        out_done = sem("h_out")
        raw = s.enter_context(nc.sbuf_tensor("h_raw", [P, 3, TILES], I32))
        onelo = s.enter_context(nc.sbuf_tensor("h_onelo", [P, 4, LO], BF16))
        onehi = s.enter_context(nc.sbuf_tensor("h_onehi", [P, 4, HI], BF16))
        cnt = [s.enter_context(nc.psum_tensor(f"h_cnt{k}", [P, 512], F32)) for k in range(2)]
        block = s.enter_context(nc.Block())
        V = 4

        @block.sync
        def _(sp):
            for k, a in enumerate((src, dst, relation)):
                sp.dma_start(raw[:, k, :], a).then_inc(loaded, 16)
            sp.wait_ge(loaded, 48)

        @block.vector
        def _(dve):
            ch = Chain(dve, chain)
            dve.wait_ge(loaded, 48)
            nc.vector.memset(onehi[:, 0, :], 0.0).then_inc(packed, 1)
            ch.link(nc.vector.memset(c.rec[:, :, 3], 0))
            for k in range(3):
                ch.link(nc.vector.tensor_copy(c.rec[:, :, k], raw[:, k, :]))
            split_digits(nc.vector, ch, c)
            dve.wait_ge(packed, 2)
            with dve.Fori(0, TILES // V) as g:
                for u in range(V):
                    dve.wait_ge(counted, g * V + u + 1)
                    nc.vector.tensor_scalar(onelo[:, u, :], c.count16[:, 0:LO], c.lo[:, bass.ds(g * V + u, 1)], None,
                                            ALU.is_equal)
                    nc.vector.tensor_scalar(onehi[:, u, :], c.count16[:], c.hi[:, bass.ds(g * V + u, 1)], None,
                                            ALU.is_equal).then_inc(ready, 1)
            dve.wait_ge(counted, TILES + V)
            for k in range(2):
                nc.vector.tensor_copy(c.hist[:, k, :], cnt[k][:, 0:HI]).then_inc(chain, 1)

        @block.tensor
        def _(pe):
            pe.wait_ge(packed, 1)
            for k in range(2):
                last = nc.tensor.matmul(cnt[k][:, 0:HI], c.ones16[:], onehi[:, 0, :], start=True, stop=False,
                                        skip_group_check=True)
            last.then_inc(packed, 1)
            pe.sem_inc(counted, V)
            with pe.Fori(0, TILES // V) as g:
                for u in range(V):
                    pe.wait_ge(ready, g * V + u + 1)
                    for k in range(2):
                        last = nc.tensor.matmul(cnt[k][:, 0:HI], onelo[:, u, k * P:(k + 1) * P], onehi[:, u, :],
                                                start=False, stop=False, skip_group_check=True)
                    last.then_inc(counted, 1)


def node_table(nc, c, table):
    with Phase(nc) as s:
        sem = lambda n: s.semaphore(n)
        chain, summed, placed, turned, taken, stored = (sem("n_chain"), sem("n_summed"), sem("n_placed"), sem("n_turned"),
                                                        sem("n_taken"), sem("n_stored"))
        first = s.enter_context(nc.sbuf_tensor("n_first", [P, 2, HI], F32))
        total = s.enter_context(nc.sbuf_tensor("n_total", [P, HI], F32))
        rows = s.enter_context(nc.sbuf_tensor("n_rows", [P, 2], F32))
        rowsb = s.enter_context(nc.sbuf_tensor("n_rowsb", [P, 2, P], F32))
        zero = s.enter_context(nc.sbuf_tensor("n_zero", [P, HI], F32))
        out = s.enter_context(nc.sbuf_tensor("n_out", [P, 4, LO, 2], I32))
        ps_tot = s.enter_context(nc.psum_tensor("n_pstot", [P, 512], F32))
        ps_f = [s.enter_context(nc.psum_tensor(f"n_psf{k}", [P, 512], F32)) for k in range(2)]
        ps_off = s.enter_context(nc.psum_tensor("n_psoff", [P, 512], F32))
        ps_t = [s.enter_context(nc.psum_tensor(f"n_pst{k}", [P, 512], F32)) for k in range(2)]
        block = s.enter_context(nc.Block())
        CH = [(h, min(P, HI - h)) for h in range(0, HI, P)]

        @block.vector
        def _(dve):
            ch = Chain(dve, chain)
            nc.vector.memset(zero[:], 0.0)
            for k in range(2):
                ch.link(nc.vector.tensor_reduce(rows[:, k:k + 1], c.hist[:, k, :], axis=AX.X, op=ALU.add))
            for k in range(2):
                ch.link(nc.vector.tensor_copy(rowsb[:, k, :], rows[:, k:k + 1].broadcast_to([P, P])))
            nc.vector.memset(c.row1f[:], 1.0).then_inc(placed, 1)
            dve.wait_ge(summed, 1)
            ch.link(nc.vector.tensor_copy(total[:], ps_tot[:, 0:HI]))
            ch.link(nc.vector.tensor_tensor_scan(c.off_hi[:], total[:], zero[:], 0.0, ALU.add, ALU.add))
            ch.link(nc.vector.tensor_tensor(c.off_hi[:], c.off_hi[:], total[:], ALU.subtract))
            for k in range(2):
                ch.link(nc.vector.tensor_tensor(first[:, k, :], ps_f[k][:, 0:HI], c.off_hi[:], ALU.add))
            ch.link(nc.vector.tensor_copy(c.off_lo[:], ps_off[:, 0:LO]))
            nc.vector.memset(zero[:, 0:1], 0.0).then_inc(placed, 1)
            n = 0
            for q, (h, m) in enumerate(CH):
                for k in range(2):
                    for w in range(2):
                        dve.wait_ge(turned, n + 1)
                        nc.vector.tensor_copy(out[0:m, q, k * P:(k + 1) * P, w], ps_t[n % 2][0:m, 0:P]).then_inc(taken, 1)
                        n += 1

        @block.tensor
        def _(pe):
            pe.wait_ge(placed, 1)
            for k in range(2):
                nc.tensor.matmul(ps_tot[:, 0:HI], c.ones[:], c.hist[:, k, :], start=k == 0, stop=k == 1)
            nc.tensor.matmul(ps_f[0][:, 0:HI], c.tri[:], c.hist[:, 0, :], start=True, stop=True)
            nc.tensor.matmul(ps_f[1][:, 0:HI], c.tri[:], c.hist[:, 1, :], start=True, stop=False)
            nc.tensor.matmul(ps_f[1][:, 0:HI], c.ones[:], c.hist[:, 0, :], start=False, stop=True)
            nc.tensor.matmul(ps_off[:, 0:P], rowsb[:, 0, :], c.tri[:], start=True, stop=True)
            nc.tensor.matmul(ps_off[:, P:LO], rowsb[:, 1, :], c.tri[:], start=True, stop=False)
            nc.tensor.matmul(ps_off[:, P:LO], rowsb[:, 0, :], c.ones[:], start=False, stop=True).then_inc(summed, 1)
            pe.wait_ge(placed, 2)
            n = 0
            for q, (h, m) in enumerate(CH):
                for k in range(2):
                    for w in range(2):
                        a = (first, c.hist)[w]
                        if n >= 2:
                            pe.wait_ge(taken, n - 1)
                        nc.tensor.transpose(ps_t[n % 2][0:m, 0:P], a[:, k, h:h + m], c.ident[:]).then_inc(turned, 1)
                        n += 1

        @block.sync
        def _(sp):
            t = table.rearrange("(h l) w -> h (l w)", l=LO)
            for q, (h, m) in enumerate(CH):
                sp.wait_ge(taken, 4 * (q + 1))
                sp.dma_start(t[h:h + m, :], out[0:m, q].rearrange("h l w -> h (l w)")).then_inc(stored, 16)
            sp.wait_ge(stored, 16 * len(CH))


def gate(engine, sem, value, passed):
    engine.wait_ge(sem, value)
    engine.sem_inc(passed, 1)


class Zeros:

    def __init__(self, zero, tables, filled):
        self.zero, self.tables, self.filled = zero, tables, filled


def sort_pass(nc, c, name, digit, width, offset, records, zeros=None):
    with Phase(nc) as s:
        sem = lambda n: s.semaphore(f"{name}_{n}")
        opened, ready, ranked, read, chain, dropped = sem("opened"), sem("ready"), sem("ranked"), sem("read"), sem("chain"), sem("dropped")
        passed = sem("passed")
        staged = sem("staged")
        sent = [s.lasting(f"{name}_sent{h}") for h in range(2)]
        R = 7
        one = s.enter_context(nc.sbuf_tensor(f"{name}_one", [P, R, width], BF16))
        junk = s.enter_context(nc.sbuf_tensor(f"{name}_junk", [P, 2, width], BF16))
        pos = s.enter_context(nc.sbuf_tensor(f"{name}_pos", [P, 2, U], F32))
        posi = s.enter_context(nc.sbuf_tensor(f"{name}_posi", [P, 2, 3, U], I32))
        index = s.enter_context(nc.sbuf_tensor(f"{name}_index", [P, 2, U], I32))
        row = s.enter_context(nc.sbuf_tensor(f"{name}_row", [P, 2, U, REC], I32))
        base = [s.enter_context(nc.psum_tensor(f"{name}_base{k}", [P, 512], F32)) for k in range(2)]
        block = s.enter_context(nc.Block())
        LINKS = 2 * 4

        if zeros is not None:
            cleared, act_passed = sem("cleared"), sem("act_passed")

            @block.scalar
            def _(act):
                for part in range(2 * U):
                    last = nc.scalar.activation(zeros.zero[:, part * D:(part + 1) * D], c.ident[:], ACT.Copy, scale=0.0)
                last.then_inc(cleared, 1)
                act.wait_ge(cleared, 1)
                with act.Fori(0, STEPS) as i:
                    gate(act, sent[0], i * (16 * U), act_passed)
                    for table in zeros.tables:
                        whole = table[0:ROWS, :].rearrange("(p t) d -> p (t d)", t=TILES)
                        act.dma_start(whole[:, bass.ds(i * (2 * U * D), 2 * U * D)], zeros.zero[:]).then_inc(zeros.filled, 16)
                act.wait_ge(zeros.filled, 16 * STEPS * len(zeros.tables))

        @block.vector
        def _(dve):
            nc.vector.memset(one[:, R - 1, :], 0.0).then_inc(ready, 1)
            with dve.Fori(0, STEPS) as i:
                for h in range(2):
                    ch = Chain(dve, chain, i * LINKS + h * 4)
                    for u in range(U + 1):
                        if u < U:
                            t = i * (2 * U) + h * U + u
                            if u == 0:
                                dve.wait_ge(dropped, t)
                            nc.vector.tensor_scalar(one[:, u, :], c.count16[:, 0:width], digit[:, bass.ds(t, 1)], None,
                                                    ALU.is_equal).then_inc(ready, 1)
                        if u > 0:
                            v = u - 1
                            dve.wait_ge(ranked, i * (2 * U) + h * U + v + 1)
                            nc.vector.tensor_tensor_reduce(out=junk[:, v % 2, :], in0=base[(h * U + v) % 2][:, 0:width],
                                                           in1=one[:, v, :], scale=1.0, scalar=0.0, op0=ALU.mult,
                                                           op1=ALU.add, accum_out=pos[:, h, v:v + 1]).then_inc(read, 1)
                    dve.wait_ge(read, i * (2 * U) + (h + 1) * U)
                    ch.link(nc.vector.tensor_copy(posi[:, h, 0, :], pos[:, h, :]))
                    ch.link(nc.vector.tensor_scalar(posi[:, h, 1, :], posi[:, h, 0, :], P - 1, None, ALU.bitwise_and))
                    ch.link(nc.vector.tensor_scalar(posi[:, h, 2, :], posi[:, h, 0, :], 7, None, ALU.logical_shift_right))
                    ch.n += 1
                    dve.wait_ge(sent[h], i * (16 * U))
                    nc.vector.scalar_tensor_tensor(index[:, h, :], posi[:, h, 1, :], float(TILES), posi[:, h, 2, :],
                                                   ALU.mult, ALU.add).then_inc(chain, 1)
                    nc.vector.tensor_scalar(row[:, h, :, :], c.rec[:, bass.ds(i * (2 * U) + h * U, U), :], 0.0, None,
                                            ALU.add).then_inc(staged, 1)
                    dve.wait_ge(chain, ch.base + ch.n)

        @block.tensor
        def _(pe):
            pe.wait_ge(ready, 1)
            for k in range(2):
                nc.tensor.matmul(base[k][:, 0:width], c.row1f[:], offset[0:1, 0:width], start=True, stop=False,
                                 skip_group_check=True)
            with pe.Fori(0, STEPS) as i:
                for v in range(2 * U):
                    t = i * (2 * U) + v
                    slot, before = v % R, (v - 1) % R
                    pe.wait_ge(ready, t + 2)
                    nc.tensor.matmul(base[v % 2][:, 0:width], c.tri16[:], one[:, slot, :], start=False, stop=False,
                                     skip_group_check=True).then_inc(ranked, 1)
                    pe.wait_ge(read, t)
                    nc.tensor.matmul(base[(v + 1) % 2][:, 0:width], c.rest16[:], one[:, before, :], start=False, stop=False,
                                     skip_group_check=True).then_inc(dropped, 1)
                    nc.tensor.matmul(base[(v + 1) % 2][:, 0:width], c.ones16[:], one[:, slot, :], start=False, stop=False,
                                     skip_group_check=True)

        @block.gpsimd
        def _(pool):
            with pool.Fori(0, STEPS) as i:
                for h in range(2):
                    pool.wait_ge(staged, i * 2 + h + 1)
                    pool.sem_inc(passed, 1)
                    for u in range(U):
                        nc.gpsimd.indirect_dma_start(records, bass.IndirectOffsetOnAxis(ap=index[:, h, u:u + 1], axis=0),
                                                     row[:, h, u, :], None).then_inc(sent[h], 16)
            for h in range(2):
                pool.wait_ge(sent[h], STEPS * 16 * U)


def reload(nc, c, name, records):
    with Phase(nc) as s:
        loaded, chain = (s.semaphore(f"{name}_{n}") for n in ("loaded", "chain"))
        block = s.enter_context(nc.Block())

        @block.sync
        def _(sp):
            sp.dma_start(c.rec[:].rearrange("p t w -> p (t w)"), records.rearrange("(p t) w -> p (t w)", t=TILES)).then_inc(loaded, 16)

        @block.vector
        def _(dve):
            dve.wait_ge(loaded, 16)
            split_digits(nc.vector, Chain(dve, chain), c)


class Persistent:

    def __init__(self, nc, s):
        sb = lambda n, shape, dt=F32: s.enter_context(nc.sbuf_tensor(n, shape, dt))
        self.ident, self.ones, self.tri = sb("ident", [P, P]), sb("ones", [P, P]), sb("tri", [P, P])
        self.row_first, self.row_last = sb("row_first", [P, P]), sb("row_last", [P, P])
        self.tri16, self.rest16, self.ones16 = sb("tri16", [P, P], BF16), sb("rest16", [P, P], BF16), sb("ones16", [P, P], BF16)
        self.count16 = sb("count16", [P, HI], F16)
        self.part = sb("part", [P, 1])
        self.row1f = sb("row1f", [1, P])
        self.rec = sb("rec", [P, TILES, REC], I32)
        self.digit = sb("digit", [P, TILES], I32)
        self.lo, self.hi = sb("lo", [P, TILES]), sb("hi", [P, TILES])
        self.hist = sb("hist", [P, 2, HI])
        self.off_lo, self.off_hi = sb("off_lo", [P, LO]), sb("off_hi", [P, HI])

FAR = 1 << 20
ZERO = ROWS
EPS = 1e-5
CHUNKS = 4
TROWS = TILES // CHUNKS


def within(nc, column, last):
    if isinstance(column, int):
        return column
    return nc.s_assert_within(column, 0, last, skip_runtime_bounds_check_because="loops run over j < steps <= STEPS")


class Segments:

    def __init__(self, nc, s, name):
        sb = lambda n, shape, dt=F32: s.enter_context(nc.sbuf_tensor(f"{name}_{n}", shape, dt))
        self.src = sb("src_col", [P, TILES + 1])
        self.same_next_tile = sb("same_next_tile", [P, TILES])
        self.same_prev_tile = sb("same_prev_tile", [P, TILES])
        self.whole_next = sb("whole_next", [P, TILES])
        self.whole_prev = sb("whole_prev", [P, TILES])
        self.in_first = sb("in_first", [P, TILES], I32)
        self.like_prev = sb("like_prev", [TROWS, CHUNKS * P])
        self.like_next = sb("like_next", [TROWS, CHUNKS * P])
        self.pens = [sb(f"pen{i}", shape) for i, shape in enumerate([[TROWS, CHUNKS * P]] * 2 + [[P, TILES]] * 4)]
        self.count = sb("count", [P, TILES])
        self.root = sb("root", [P, TILES])
        self.inv_root = sb("inv_root", [P, TILES])
        self.like = sb("like", [P, TILES])
        self.place = sb("place", [P, TILES])
        self.out_index = sb("out_index", [P, TILES], I32)
        self.in_first4 = sb("in_first4", [P, 2, 4], I32)
        self.score4 = sb("score4", [P, 2, 4])
        self.top, self.scale = sb("top", [P, TILES]), sb("scale", [P, TILES])


def reversed_(ap):
    return ap[:, ::-1]


class FullEdges(Segments):

    def __init__(self, nc, s):
        super().__init__(nc, s, "full")
        sb = lambda n, shape, dt=F32: s.enter_context(nc.sbuf_tensor(f"full_{n}", shape, dt))
        self.x_index = sb("x_index", [P, TILES], I32)
        self.entity_index = sb("entity_index", [P, TILES], I32)
        self.state_index = sb("state_index", [P, TILES], I32)
        self.first_entity = sb("first_entity", [TROWS, CHUNKS], I32)
        self.dst_first = sb("dst_first", [P, TILES])
        self.live = sb("live", [P, TILES])
        self.before = sb("before", [P, TILES])
        self.before_capped = sb("before_capped", [P, TILES])
        self.has_live = sb("has_live", [P, TILES])
        self.first = sb("first", [P, TILES])


class LiveEdges(Segments):

    def __init__(self, nc, s):
        super().__init__(nc, s, "live")
        sb = lambda n, shape, dt=F32: s.enter_context(nc.sbuf_tensor(f"live_{n}", shape, dt))
        self.rec = sb("rec", [P, TILES, LIVE_REC], I32)
        self.coef = sb("coef", [P, TILES])
        self.extra = sb("extra", [P, TILES])
        self.dead = sb("dead", [P, TILES])
        self.steps = sb("steps", [1, 1], I32)
        self.turns = sb("turns", [1, 1], I32)
        names = ("dst_first", "src_first", "state_a", "state_b", "target_part", "own_part", "table_index")
        self.columns = {}
        for n in names:
            self.columns[n] = sb(n, [P, TILES], I32)


LIVE_REC = 8


def find_segments(nc, c, g, name, rec):
    with Phase(nc) as s:
        sem = lambda n: s.semaphore(f"{name}_{n}")
        chain, put, turned = sem("chain"), sem("put"), sem("turned")
        src_t = s.enter_context(nc.sbuf_tensor(f"{name}_srct", [TROWS, CHUNKS * P], F32))
        first = s.enter_context(nc.sbuf_tensor(f"{name}_first", [P, TILES], F32))
        last_ = s.enter_context(nc.sbuf_tensor(f"{name}_last", [P, TILES], F32))
        zero_row = s.enter_context(nc.sbuf_tensor(f"{name}_zero_row", [P, 1], F32))
        pa, pb, pt, pl = (s.enter_context(nc.psum_tensor(f"{name}_p{i}", [P, 512], F32)) for i in range(4))
        block = s.enter_context(nc.Block())

        @block.vector
        def _(dve):
            ch = Chain(dve, chain)
            v = nc.vector
            ch.link(v.tensor_copy(g.src[:, 0:TILES], rec[:, :, 0]))
            v.memset(g.src[:, TILES:TILES + 1], -1.0).then_inc(put, 1)
            ch.link(v.tensor_scalar(zero_row[:], c.part[:], 0.0, None, ALU.is_equal))
            ch.link(v.memset(g.same_next_tile[:, TILES - 1:TILES], 0.0))
            ch.link(v.memset(g.same_prev_tile[:, 0:1], 0.0))
            ch.link(v.memset(g.like_prev[:], 0.0))
            ch.link(v.memset(g.like_next[:], 0.0))
            dve.wait_ge(turned, 1)
            ch.link(v.tensor_copy(first[:], pa[:, 0:TILES]))
            ch.link(v.tensor_copy(last_[:], pb[:, 0:TILES]))
            ch.link(v.tensor_copy(src_t[:], pt[0:TROWS, :]))
            T = TILES
            ch.link(v.tensor_tensor(g.same_next_tile[:, 0:T - 1], g.src[:, 0:T - 1], first[:, 1:T], ALU.is_equal))
            ch.link(v.tensor_tensor(g.same_prev_tile[:, 1:T], g.src[:, 1:T], last_[:, 0:T - 1], ALU.is_equal))
            ch.link(v.tensor_tensor(g.in_first[:], g.src[:, 0:T], first[:], ALU.is_equal))
            st = src_t[:].rearrange("r (c j) -> r c j", j=P)
            lp = g.like_prev[:].rearrange("r (c j) -> r c j", j=P)
            ln = g.like_next[:].rearrange("r (c j) -> r c j", j=P)
            ch.link(v.tensor_tensor(lp[:, :, 1:P], st[:, :, 1:P], st[:, :, 0:P - 1], ALU.is_equal))
            ch.link(v.tensor_copy(ln[:, :, 0:P - 1], lp[:, :, 1:P]))
            v.memset(src_t[:, 0:1], 0.0).then_inc(put, 1)
            dve.wait_ge(turned, 2)
            ch.link(v.tensor_copy(g.whole_next[:], pa[:, 0:TILES]))
            ch.link(v.tensor_copy(g.whole_prev[:], pb[:, 0:TILES]))
            ch.link(v.scalar_tensor_tensor(g.like[:], g.same_prev_tile[:], zero_row[:], pl[:, 0:TILES], ALU.mult, ALU.add))
            ch.link(v.scalar_tensor_tensor(g.out_index[:], g.like[:], float(FAR), g.src[:, 0:T], ALU.mult, ALU.add))
            flags = (g.like_prev, g.like_next, g.same_next_tile, g.same_prev_tile, g.whole_next, g.whole_prev)
            for pen, flag in zip(g.pens, flags):
                ch.link(v.tensor_scalar(pen[:], flag[:], 2 * LIMIT, -LIMIT, ALU.mult, ALU.add))

        @block.tensor
        def _(pe):
            pe.wait_ge(put, 1)
            nc.tensor.matmul(pa[:, 0:TILES], c.row_first[:], g.src[:, 0:TILES], start=True, stop=True)
            nc.tensor.matmul(pb[:, 0:TILES], c.row_last[:], g.src[:, 0:TILES], start=True, stop=True)
            for q in range(CHUNKS):
                last = nc.tensor.transpose(pt[0:TROWS, q * P:(q + 1) * P], g.src[:, q * TROWS:(q + 1) * TROWS], c.ident[:])
            last.then_inc(turned, 1)
            pe.wait_ge(put, 2)
            nc.tensor.matmul(pa[:, 0:TILES], c.row_first[:], g.same_next_tile[:], start=True, stop=True)
            nc.tensor.matmul(pb[:, 0:TILES], c.row_last[:], g.same_prev_tile[:], start=True, stop=True)
            for q in range(CHUNKS):
                last = nc.tensor.transpose(pl[:, q * TROWS:(q + 1) * TROWS], g.like_prev[:, q * P:(q + 1) * P],
                                           c.ident[0:TROWS, 0:TROWS])
            last.then_inc(turned, 1)


LIMIT = 1.0e38


def segment_reduce(nc, c, g, name, a, out, op):
    with Phase(nc) as s:
        sem = lambda n: s.semaphore(f"{name}_{n}")
        chain, put, turned = sem("chain"), sem("put"), sem("turned")
        at, fw, bw = (s.enter_context(nc.sbuf_tensor(f"{name}_s{i}", [TROWS, CHUNKS * P], F32)) for i in range(3))
        edge = s.enter_context(nc.sbuf_tensor(f"{name}_edge", [P, TILES], F32))
        carry = s.enter_context(nc.sbuf_tensor(f"{name}_carry", [P, TILES + 1], F32))
        tmp = s.enter_context(nc.sbuf_tensor(f"{name}_tmp", [P, TILES], F32))
        pt, pr, pe_, pl = (s.enter_context(nc.psum_tensor(f"{name}_p{i}", [P, 512], F32)) for i in range(4))
        block = s.enter_context(nc.Block())
        T = TILES
        if op == ALU.add:
            keep, join, none = ALU.mult, ALU.add, 0.0
            prev, nxt, into_next, into_prev, over_next, over_prev = (g.like_prev, g.like_next, g.same_next_tile,
                                                                     g.same_prev_tile, g.whole_next, g.whole_prev)
        else:
            keep, join, none = ALU.min, ALU.max, -LIMIT
            prev, nxt, into_next, into_prev, over_next, over_prev = g.pens

        @block.vector
        def _(dve):
            ch = Chain(dve, chain)
            v = nc.vector
            dve.wait_ge(turned, 1)
            ch.link(v.tensor_copy(at[:], pt[0:TROWS, :]))
            ch.link(v.tensor_tensor_scan(fw[:], prev[:], at[:], none, keep, join))
            ch.link(v.tensor_tensor_scan(reversed_(bw[:]), reversed_(nxt[:]), reversed_(at[:]), none, keep, join))
            ch.link(v.tensor_tensor(fw[:], fw[:], bw[:], join))
            if op == ALU.add:
                ch.link(v.tensor_tensor(fw[:], fw[:], at[:], ALU.subtract))
            v.memset(carry[:], none).then_inc(put, 1)
            dve.wait_ge(turned, 2)
            ch.link(v.tensor_copy(out[:], pr[:, 0:T]))
            v.memset(bw[:, 0:1], 0.0).then_inc(put, 1)
            dve.wait_ge(turned, 3)
            ch.link(v.tensor_copy(edge[:], pe_[:, 0:T]))
            ch.link(v.tensor_tensor_scan(reversed_(carry[:, 0:T]), reversed_(over_next[:]), reversed_(edge[:]), none, keep, join))
            ch.link(v.tensor_tensor(tmp[:], into_next[:], carry[:, 1:T + 1], keep))
            ch.link(v.tensor_tensor(out[:], out[:], tmp[:], join))
            if op != ALU.add:
                v.memset(bw[:, 0:1], 0.0).then_inc(put, 1)
                dve.wait_ge(turned, 4)
                ch.link(v.tensor_copy(edge[:], pl[:, 0:T]))
                ch.link(v.memset(carry[:, 0:1], none))
                ch.link(v.tensor_tensor_scan(carry[:, 1:T + 1], over_prev[:], edge[:], none, keep, join))
                ch.link(v.tensor_tensor(tmp[:], into_prev[:], carry[:, 0:T], keep))
                ch.link(v.tensor_tensor(out[:], out[:], tmp[:], join))

        @block.tensor
        def _(pe):
            for q in range(CHUNKS):
                last = nc.tensor.transpose(pt[0:TROWS, q * P:(q + 1) * P], a[:, q * TROWS:(q + 1) * TROWS], c.ident[:])
            last.then_inc(turned, 1)
            pe.wait_ge(put, 1)
            for q in range(CHUNKS):
                last = nc.tensor.transpose(pr[:, q * TROWS:(q + 1) * TROWS], fw[:, q * P:(q + 1) * P],
                                           c.ident[0:TROWS, 0:TROWS])
            last.then_inc(turned, 1)
            pe.wait_ge(put, 2)
            nc.tensor.matmul(pe_[:, 0:T], c.row_first[:], out[:], start=True, stop=True).then_inc(turned, 1)
            if op != ALU.add:
                pe.wait_ge(put, 3)
                nc.tensor.matmul(pl[:, 0:T], c.row_last[:], out[:], start=True, stop=True).then_inc(turned, 1)


def simple(nc, name, vector_steps, scalar_step=None):
    with Phase(nc) as s:
        chain, asked, done = (s.semaphore(f"{name}_{n}") for n in ("chain", "asked", "done"))
        block = s.enter_context(nc.Block())

        @block.vector
        def _(dve):
            ch = Chain(dve, chain)
            for step in vector_steps:
                if step is None:
                    dve.sem_inc(asked, 1)
                    dve.wait_ge(done, 1)
                else:
                    ch.link(step(nc.vector))

        if scalar_step is not None:
            @block.scalar
            def _(act):
                act.wait_ge(asked, 1)
                scalar_step(nc.scalar).then_inc(done, 1)


class Marks(Chain):

    def mark(self, instruction):
        self.n += 1
        instruction.then_inc(self.sem, 1)

    def wait(self):
        self.engine.wait_ge(self.sem, self.base + self.n)


def halves(s, nc, name):
    return [s.semaphore(f"{name}{h}") for h in range(2)]


def lasting_halves(s, name):
    return [s.lasting(f"{name}{h}") for h in range(2)]


def row_stats(v, ch, passed, stat, mv, var, rows, n, mv_n):
    for u in range(n):
        ch.mark(v.bn_stats(stat[:, u, :], rows[:, u, :]))
    gate(ch.engine, ch.sem, ch.base + ch.n, passed)
    for u in range(n):
        ch.mark(v.bn_aggr(mv[:, u, :], stat[:, u, :]))
    ch.wait()
    return v.tensor_scalar(var, mv_n[:, :, 1], EPS, None, ALU.add)


def rows_of(table, first, n):
    return table[bass.ds(first, n * P), :].rearrange("(u p) d -> p u d", p=P)


DENSE_P = 125
DENSE_ROWS = NODES // DENSE_P
DENSE_N = 14
DENSE_TAIL = DENSE_ROWS - 2 * STEPS * DENSE_N


class Dense:

    def __init__(self, nc, s, x, entity, out):
        self.nc = nc
        view = lambda a: a.rearrange("(p n) d -> p n d", p=DENSE_P)
        self.x, self.entity, self.out = view(x), view(entity[0:NODES, :]), view(out)
        (self.loaded, self.links, self.varied, self.rooted, self.steadied, self.normed, self.finished, self.stored) = (
            halves(s, nc, f"dense_{n}") for n in ("loaded", "links", "varied", "rooted", "steadied", "normed", "finished", "stored"))
        self.act_passed, self.dve_passed, self.sp_passed = (s.semaphore(f"dense_{n}")
                                                            for n in ("act_passed", "dve_passed", "sp_passed"))
        n = max(DENSE_N, DENSE_TAIL)
        sb = lambda name, shape: s.enter_context(nc.sbuf_tensor(f"dense_{name}", shape, F32))
        self.rows, self.norm, self.result = (sb(k, [DENSE_P, 2, n, D]) for k in ("rows", "norm", "result"))
        self.stat, self.mv = sb("stat", [DENSE_P, 2, n, 6]), sb("mv", [DENSE_P, 2, n, 2])
        self.var, self.root, self.inv, self.shift = (sb(k, [DENSE_P, 2, n]) for k in ("var", "root", "inv", "shift"))

    def links_from(self, dve, k, h, done):
        return Marks(dve, self.links[h], k * (4 * DENSE_N + 3) + done)

    def load(self, sp, k, h, first, n):
        gate(sp, self.finished[h], k, self.sp_passed)
        sp.dma_start(self.rows[:, h, 0:n, :], self.x[:, bass.ds(first, n), :]).then_inc(self.loaded[h], 16)

    def stats(self, dve, k, h, n, second, loads=None):
        ch = self.links_from(dve, k, h, second * (2 * n + 1))
        v = self.nc.vector
        if second:
            dve.wait_ge(self.normed[h], k * 2 + 1)
            ch.link(v.scalar_tensor_tensor(self.rows[:, h, 0:n, :], self.norm[:, h, 0:n, :], 0.1, self.rows[:, h, 0:n, :],
                                           ALU.mult, ALU.add))
        else:
            gate(dve, self.loaded[h], (k + 1 if loads is None else loads) * 16, self.dve_passed)
        row_stats(v, ch, self.dve_passed, self.stat[:, h], self.mv[:, h], self.var[:, h, 0:n], self.rows[:, h],
                  n, self.mv[:, h, 0:n]).then_inc(self.varied[h], 1)

    def scale(self, dve, k, h, n, second):
        v = self.nc.vector
        dve.wait_ge(self.rooted[h], k * 2 + 1 + second)
        ch = self.links_from(dve, k, h, 2 * n + second * (2 * n + 2))
        ch.link(v.reciprocal(self.inv[:, h, 0:n], self.root[:, h, 0:n]))
        v.scalar_tensor_tensor(self.shift[:, h, 0:n], self.mv[:, h, 0:n, 0], -1.0, self.inv[:, h, 0:n], ALU.mult,
                               ALU.mult).then_inc(self.steadied[h], 1)

    def finish(self, dve, turns_done, h, n):
        dve.wait_ge(self.normed[h], turns_done * 2)
        self.nc.vector.scalar_tensor_tensor(self.result[:, h, 0:n, :], self.norm[:, h, 0:n, :], 3.0, self.rows[:, h, 0:n, :],
                                            ALU.mult, ALU.add).then_inc(self.finished[h], 1)

    def take_root(self, act, k, h, n, second):
        act.wait_ge(self.varied[h], k * 2 + 1 + second)
        self.nc.scalar.activation(self.root[:, h, 0:n], self.var[:, h, 0:n], ACT.Sqrt).then_inc(self.rooted[h], 1)

    def normalise(self, act, k, h, n, second):
        if not second:
            gate(act, self.stored[h], k * 32, self.act_passed)
        act.wait_ge(self.steadied[h], k * 2 + 1 + second)
        for u in range(n):
            last = self.nc.scalar.activation(self.norm[:, h, u, :], self.rows[:, h, u, :], ACT.Relu,
                                             bias=self.shift[:, h, u:u + 1], scale=self.inv[:, h, u:u + 1])
        last.then_inc(self.normed[h], 1)

    def store(self, sp, k, h, first, n):
        gate(sp, self.normed[h], k * 2 + 2, self.sp_passed)
        sp.dma_start(self.entity[:, bass.ds(first, n), :], self.norm[:, h, 0:n, :]).then_inc(self.stored[h], 16)
        gate(sp, self.finished[h], k + 1, self.sp_passed)
        sp.dma_start(self.out[:, bass.ds(first, n), :], self.result[:, h, 0:n, :]).then_inc(self.stored[h], 16)


def edge_info(nc, c, g, x, table, sorted_rows, x_rows, g0_rows, states, entity, out):
    with Phase(nc) as s:
        sem = lambda n: s.semaphore(f"e_{n}")
        passed, act_passed, dve_passed, sp_passed, copied, first_loaded, chain = (
            sem(n) for n in ("passed", "act_passed", "dve_passed", "sp_passed", "copied", "first_loaded", "chain"))
        first_done, gathered = s.lasting("e_first_done"), lasting_halves(s, "e_gathered")
        links, varied, rooted, steadied, scaled, cut, taken, x_stored, g_stored = (
            halves(s, nc, f"e_{n}") for n in ("links", "varied", "rooted", "steadied", "scaled", "cut", "taken", "x_stored", "g_stored"))
        sb = lambda n, shape, dt=F32: s.enter_context(nc.sbuf_tensor(f"e_{n}", shape, dt))
        ix, it = sb("ix", [P, 2, U], I32), sb("it", [P, 2, U], I32)
        xg, tg = sb("xg", [P, 2, U, D]), sb("tg", [P, 2, U, 2], I32)
        g0 = sb("g0", [P, 2, U, D])
        stat, mv = sb("stat", [P, 2, U, 6]), sb("mv", [P, 2, U, 2])
        var, inv, root, shift = sb("var", [P, 2, U]), sb("inv", [P, 2, U]), sb("root", [P, 2, U]), sb("shift", [P, 2, U])
        dst_degree, away = sb("dst_degree", [P, TILES]), sb("away", [P, TILES])
        tenth = sb("tenth", [P, 2, U, D])
        first_rec, first_tab = sb("first_rec", [TROWS, CHUNKS, REC], I32), sb("first_tab", [TROWS, CHUNKS, 2], I32)
        dense = Dense(nc, s, x, entity, out)
        block = s.enter_context(nc.Block())
        K = 2 * U + 2

        @block.vector
        def _(dve):
            v = nc.vector

            def edge_stats(i, h):
                ch = Marks(dve, links[h], i * K)
                t = i * (2 * U) + h * U
                dve.wait_ge(gathered[h], (i + 1) * (32 * U))
                v.tensor_scalar(g.dst_first[:, bass.ds(t, U)], tg[:, h, :, 0], 0.0, None, ALU.add)
                v.tensor_scalar(dst_degree[:, bass.ds(t, U)], tg[:, h, :, 1], 0.0, None, ALU.add).then_inc(taken[h], 1)
                row_stats(v, ch, dve_passed, stat[:, h], mv[:, h], var[:, h, :], xg[:, h], U, mv[:, h]).then_inc(varied[h], 1)

            def edge_scale(i, h):
                ch = Marks(dve, links[h], i * K + 2 * U)
                t = i * (2 * U) + h * U
                dve.wait_ge(rooted[h], i + 1)
                dve.wait_ge(scaled[h], i)
                ch.link(v.reciprocal(inv[:, h, :], root[:, h, :]))
                ch.link(v.tensor_tensor(inv[:, h, :], inv[:, h, :], g.inv_root[:, bass.ds(t, U)], ALU.mult))
                v.scalar_tensor_tensor(shift[:, h, :], mv[:, h, :, 0], -1.0, inv[:, h, :], ALU.mult, ALU.mult).then_inc(steadied[h], 1)

            with dve.Fori(0, STEPS) as i:
                for h in range(2):
                    dense.stats(dve, i, h, DENSE_N, 0)
                    dense.scale(dve, i, h, DENSE_N, 0)
                    if h == 0:
                        with dve.If(i > 0):
                            dense.finish(dve, i, 1, DENSE_N)
                    else:
                        dve.wait_ge(dense.stored[0], i * 32)
                        dense.finish(dve, i + 1, 0, DENSE_N)
                    edge_stats(i, h)
                    dense.stats(dve, i, h, DENSE_N, 1)
                    dense.scale(dve, i, h, DENSE_N, 1)
                    edge_scale(i, h)
                gate(dve, dense.stored[1], i * 32, dve_passed)
            dense.finish(dve, STEPS, 1, DENSE_N)
            for second in range(2):
                dense.stats(dve, STEPS, 0, DENSE_TAIL, second, loads=STEPS + 2)
                dense.scale(dve, STEPS, 0, DENSE_TAIL, second)
            dve.wait_ge(dense.stored[0], STEPS * 32)
            dense.finish(dve, STEPS + 1, 0, DENSE_TAIL)
            for h in range(2):
                dve.wait_ge(taken[h], STEPS)
            ch = Chain(dve, chain)
            ch.link(v.tensor_scalar(g.live[:], dst_degree[:], 0.0, None, ALU.is_gt))
            ch.link(v.tensor_scalar(away[:], g.dst_first[:], float(NODES), None, ALU.add))
            ch.link(v.tensor_tensor(away[:], away[:], c.rec[:, :, 1], ALU.subtract))
            ch.link(v.tensor_tensor(away[:], away[:], g.live[:], ALU.mult))
            ch.link(v.tensor_tensor(g.entity_index[:], away[:], c.rec[:, :, 1], ALU.add))
            ch.link(v.tensor_scalar(away[:], g.src[:, 0:TILES], float(NODES), None, ALU.is_lt))
            ch.link(v.tensor_tensor(g.live[:], g.live[:], away[:], ALU.mult))
            dve.wait_ge(first_done, 16 * CHUNKS)
            ch.link(v.tensor_scalar(g.first_entity[:], first_tab[:, :, 0], float(NODES), None, ALU.add))

        @block.scalar
        def _(act):
            def edge_root(i, h):
                act.wait_ge(varied[h], i + 1)
                nc.scalar.activation(root[:, h, :], var[:, h, :], ACT.Sqrt).then_inc(rooted[h], 1)

            def edge_rows(i, h):
                gate(act, g_stored[h], i * 32, act_passed)
                act.wait_ge(steadied[h], i + 1)
                for u in range(U):
                    last = nc.scalar.activation(g0[:, h, u, :], xg[:, h, u, :], ACT.Relu, bias=shift[:, h, u:u + 1],
                                                scale=inv[:, h, u:u + 1])
                last.then_inc(scaled[h], 1)
                act.wait_ge(scaled[h], i + 1)
                nc.scalar.activation(tenth[:, h], g0[:, h], ACT.Copy, scale=0.1).then_inc(cut[h], 1)

            with act.Fori(0, STEPS) as i:
                for h in range(2):
                    dense.take_root(act, i, h, DENSE_N, 0)
                    dense.normalise(act, i, h, DENSE_N, 0)
                    edge_root(i, h)
                    dense.take_root(act, i, h, DENSE_N, 1)
                    dense.normalise(act, i, h, DENSE_N, 1)
                    edge_rows(i, h)
            for second in range(2):
                dense.take_root(act, STEPS, 0, DENSE_TAIL, second)
                dense.normalise(act, STEPS, 0, DENSE_TAIL, second)

        @block.gpsimd
        def _(pool):
            pool.wait_ge(first_loaded, 16)
            for q in range(CHUNKS):
                nc.gpsimd.indirect_dma_start(first_tab[:, q, :], None, table,
                                             bass.IndirectOffsetOnAxis(ap=first_rec[:, q, 0:1], axis=0)).then_inc(first_done, 16)
            with pool.Fori(0, STEPS) as i:
                for h in range(2):
                    t = i * (2 * U) + h * U
                    gate(pool, x_stored[h], i * 16, passed)
                    gate(pool, scaled[h], i, passed)
                    gate(pool, taken[h], i, passed)
                    nc.gpsimd.tensor_copy(ix[:, h, :], g.x_index[:, bass.ds(t, U)]).then_inc(copied, 1)
                    nc.gpsimd.tensor_copy(it[:, h, :], c.rec[:, bass.ds(t, U), 1]).then_inc(copied, 1)
                    gate(pool, copied, i * 4 + 2 * h + 2, passed)
                    for u in range(U):
                        nc.gpsimd.indirect_dma_start(xg[:, h, u, :], None, x,
                                                     bass.IndirectOffsetOnAxis(ap=ix[:, h, u:u + 1], axis=0)).then_inc(gathered[h], 16)
                        nc.gpsimd.indirect_dma_start(tg[:, h, u, :], None, table,
                                                     bass.IndirectOffsetOnAxis(ap=it[:, h, u:u + 1], axis=0)).then_inc(gathered[h], 16)

        @block.sync
        def _(sp):
            sp.dma_start(first_rec[:], sorted_rows[0:TILES, :].rearrange("(q r) w -> r q w", r=TROWS)).then_inc(first_loaded, 16)
            for h in range(2):
                dense.load(sp, 0, h, h * DENSE_N, DENSE_N)
            with sp.Fori(0, STEPS) as i:
                for h in range(2):
                    t = i * (2 * U) + h * U
                    sp.wait_ge(gathered[h], (i + 1) * (32 * U))
                    sp.dma_start(rows_of(x_rows, t * P, U), xg[:, h]).then_inc(x_stored[h], 16)
                    sp.wait_ge(scaled[h], i + 1)
                    sp.dma_start(rows_of(g0_rows, t * P, U), g0[:, h]).then_inc(g_stored[h], 16)
                    gate(sp, cut[h], i + 1, sp_passed)
                    sp.dma_start(rows_of(states, 2 * ROWS + t * P, U), tenth[:, h]).then_inc(g_stored[h], 16)
                    dense.load(sp, i + 1, h, ((i + 1) % STEPS) * (2 * DENSE_N) + h * DENSE_N, DENSE_N)
                    dense.store(sp, i, h, i * (2 * DENSE_N) + h * DENSE_N, DENSE_N)
            for h in range(2):
                sp.wait_ge(dense.loaded[h], (STEPS + 1) * 16)
            dense.load(sp, STEPS, 0, 2 * STEPS * DENSE_N, DENSE_TAIL)
            dense.store(sp, STEPS, 0, 2 * STEPS * DENSE_N, DENSE_TAIL)
            for h in range(2):
                sp.wait_ge(x_stored[h], STEPS * 16)
                sp.wait_ge(g_stored[h], STEPS * 32)
                sp.wait_ge(dense.stored[h], STEPS * 32 + (32 if h == 0 else 0))


def zero_rows(nc, tables):
    with Phase(nc) as s:
        zeroed, stored = s.semaphore("z_zeroed"), s.semaphore("z_stored")
        zero = s.enter_context(nc.sbuf_tensor("z_zero", [1, D], F32))
        block = s.enter_context(nc.Block())

        @block.vector
        def _(dve):
            nc.vector.memset(zero[:], 0.0).then_inc(zeroed, 1)

        @block.sync
        def _(sp):
            sp.wait_ge(zeroed, 1)
            for t in tables:
                sp.dma_start(t[ZERO:ZERO + 1, :], zero[:]).then_inc(stored, 16)
            sp.wait_ge(stored, 16 * len(tables))


def propagate(nc, c, g, name, g0_rows, states, live_g0, hops):
    with Phase(nc) as s:
        sem = lambda n: s.semaphore(f"{name}_{n}")
        copied, passed, sp_passed, act_passed, dve_passed, opened = (
            sem(n) for n in ("copied", "passed", "sp_passed", "act_passed", "dve_passed", "opened"))
        staged, spread, matched, summed, handed, completed, evacuated, blended, loaded, stored = (
            halves(s, nc, f"{name}_{n}") for n in ("staged", "spread", "matched", "summed", "handed", "completed", "evacuated", "blended", "loaded", "stored"))
        gathered = lasting_halves(s, f"{name}_gathered")
        sb = lambda n, shape, dt=F32: s.enter_context(nc.sbuf_tensor(f"{name}_{n}", shape, dt))
        index = sb("index", [P, 2, U], I32)
        cols = sb("cols", [P, 2, U + 1])
        got, base = sb("got", [P, 2, U, D]), sb("base", [P, 2, U, D])
        same, into = sb("same", [P, 2, U, P]), sb("into", [1, 2, U, P])
        carry = sb("carry", [1, 2, U, D])
        new, fresh = sb("new", [P, 2, U, D]), sb("fresh", [P, 2, U, D])
        src_ps = s.enter_context(nc.psum_tensor(f"{name}_src", [P, 8, P], F32))
        sum_ps = [s.enter_context(nc.psum_tensor(f"{name}_sum{h}", [P, 8, P], F32)) for h in range(2)]
        block = s.enter_context(nc.Block())
        odd, even = states[0:ROWS, :], states[ROWS:2 * ROWS, :]

        def column(steps, j, h):
            return within(nc, steps * (2 * U) - U - j * (2 * U) - h * U, TILES - U)

        def turns(engine):
            steps = live_steps(engine, g)
            with engine.Fori(0, hops) as r:
                with engine.Fori(0, STEPS) as j:
                    with engine.If(j < steps):
                        yield steps, r * steps + j, j

        def behind(h, u):
            return carry[:, h, u + 1, :] if u < U - 1 else carry[:, 1 - h, 0, :]

        @block.vector
        def _(dve):
            v = nc.vector

            def stage(col, n, h):
                dve.wait_ge(spread[h], n)
                v.tensor_scalar(cols[:, h, :], g.src[:, bass.ds(col, U + 1)], 0.0, None, ALU.add).then_inc(staged[h], 1)

            def match(n, h):
                dve.wait_ge(staged[h], n + 1)
                dve.wait_ge(spread[h], n + 1)
                dve.wait_ge(completed[h], n)
                v.tensor_tensor(same[:, h], src_ps[:, 0:U, :], cols[:, h, 0:U].unsqueeze(2).broadcast_to([P, U, P]), ALU.is_equal)
                v.tensor_tensor(into[:, h], src_ps[0:1, 0:U, :], cols[0:1, h, 1:U + 1].unsqueeze(2).broadcast_to([1, U, P]),
                                ALU.is_equal).then_inc(matched[h], 1)

            def chain(col, n, h):
                dve.wait_ge(summed[h], n + 1)
                dve.wait_ge(completed[1 - h], n + h)
                for u in reversed(range(U)):
                    v.scalar_tensor_tensor(carry[:, h, u, :], behind(h, u), g.whole_next[0:1, bass.ds(col + u, 1)],
                                           sum_ps[h][0:1, u, :], ALU.mult, ALU.add).then_inc(handed[h], 1)
                    dve.wait_ge(handed[h], n * U + (U - u))

            def blend(turns_done, h):
                dve.wait_ge(loaded[h], turns_done * 16)
                dve.wait_ge(evacuated[h], turns_done)
                v.scalar_tensor_tensor(new[:, h], base[:, h], 0.1, fresh[:, h], ALU.mult, ALU.add).then_inc(blended[h], 1)

            v.memset(carry[:], 0.0).then_inc(opened, 1)
            dve.wait_ge(opened, 1)
            steps = live_steps(dve, g)
            stage(column(steps, 0, 0), 0, 0)
            match(0, 0)
            for steps, n, j in turns(dve):
                for h in range(2):
                    stage(column(steps, (j + h) % steps, 1 - h), n + h, 1 - h)
                    chain(column(steps, j, h), n, h)
                    match(n + h, 1 - h)
                    if h == 0:
                        with dve.If(j > 0):
                            blend(n, 1)
                    else:
                        dve.wait_ge(stored[0], n * 16)
                        blend(n + 1, 0)
                gate(dve, stored[1], n * 16, dve_passed)
                with dve.If(j + 2 > steps):
                    blend(n + 1, 1)

        @block.tensor
        def _(pe):
            def spread_sources(n, h):
                pe.wait_ge(staged[h], n + 1)
                pe.wait_ge(matched[1 - h], n + h)
                for u in range(U):
                    last = nc.tensor.transpose(src_ps[:, u, :], cols[:, h, u:u + 1].broadcast_to([P, P]), c.ident[:])
                last.then_inc(spread[h], 1)

            spread_sources(0, 0)
            for steps, n, j in turns(pe):
                for h in range(2):
                    pe.wait_ge(matched[h], n + 1)
                    pe.wait_ge(gathered[h], (n + 1) * (16 * U))
                    pe.wait_ge(evacuated[h], n)
                    for u in range(U):
                        last = nc.tensor.matmul(sum_ps[h][:, u, :], same[:, h, u, :], got[:, h, u, :],
                                                start=u % 4 == 0, stop=False, skip_group_check=True)
                    last.then_inc(summed[h], 1)
                    spread_sources(n + h, 1 - h)
                    pe.wait_ge(handed[h], (n + 1) * U)
                    for u in range(U):
                        last = nc.tensor.matmul(sum_ps[h][:, u, :], into[:, h, u, :], behind(h, u), start=False, stop=u in (3, U - 1),
                                                skip_group_check=True)
                    last.then_inc(completed[h], 1)

        @block.scalar
        def _(act):
            for steps, n, j in turns(act):
                for h in range(2):
                    gate(act, blended[h], n, act_passed)
                    gate(act, completed[h], n + 1, act_passed)
                    for u in range(U):
                        last = nc.scalar.activation(fresh[:, h, u, :], sum_ps[h][:, u, :], ACT.Copy,
                                                    scale=g.coef[:, bass.ds(column(steps, j, h) + u, 1)])
                    last.then_inc(evacuated[h], 1)

        @block.gpsimd
        def _(pool):
            steps = live_steps(pool, g)

            def hop(number, source, where):
                for h in range(2):
                    gate(pool, stored[h], number * steps * 16, passed)
                with pool.Fori(0, STEPS) as j:
                    with pool.If(j < steps):
                        n = number * steps + j
                        for h in range(2):
                            gate(pool, summed[h], n, passed)
                            nc.gpsimd.tensor_copy(index[:, h, :], g.columns[where][:, bass.ds(column(steps, j, h), U)]).then_inc(copied, 1)
                            gate(pool, copied, n * 2 + h + 1, passed)
                            for u in range(U):
                                nc.gpsimd.indirect_dma_start(got[:, h, u, :], None, source,
                                                             bass.IndirectOffsetOnAxis(ap=index[:, h, u:u + 1], axis=0)).then_inc(gathered[h], 16)

            hop(0, g0_rows, "dst_first")
            hop(1, states, "state_a")
            with pool.Fori(1, hops // 2) as r:
                hop(r * 2, states, "state_b")
                hop(r * 2 + 1, states, "state_a")

        @block.sync
        def _(sp):
            steps = live_steps(sp, g)
            with sp.Fori(0, hops // 2) as r:
                for k, target in enumerate((odd, even)):
                    with sp.Fori(0, STEPS) as j:
                        with sp.If(j < steps):
                            n = (r * 2 + k) * steps + j
                            for h in range(2):
                                gate(sp, blended[h], n, sp_passed)
                                sp.dma_start(base[:, h], rows_of(live_g0, column(steps, j, h) * P, U)).then_inc(loaded[h], 16)
                            for h in range(2):
                                gate(sp, blended[h], n + 1, sp_passed)
                                sp.dma_start(rows_of(target, column(steps, j, h) * P, U), new[:, h]).then_inc(stored[h], 16)
            for h in range(2):
                gate(sp, stored[h], steps * (hops * 16), sp_passed)


def live_steps(engine, g):
    return engine.value_load(g.steps[0:1, 0:1], min_val=1, max_val=STEPS)

V = 4
TURNS = TILES // (2 * V)


def second_norm(nc, c, g, x_rows, states, entity_rows, kept):
    with Phase(nc) as s:
        sem = lambda n: s.semaphore(f"s_{n}")
        act_passed, dve_passed, sp_passed, passed, copied = (
            sem(n) for n in ("act_passed", "dve_passed", "sp_passed", "passed", "copied"))
        gathered = lasting_halves(s, "s_gathered")
        index = s.enter_context(nc.sbuf_tensor("s_index", [P, 2, U], I32))
        loaded, links, varied, rooted, steadied, normed, finished, stored = (
            halves(s, nc, f"s_{n}") for n in ("loaded", "links", "varied", "rooted", "steadied", "normed", "finished", "stored"))
        sb = lambda n, shape, dt=F32: s.enter_context(nc.sbuf_tensor(f"s_{n}", shape, dt))
        xr, st, ent, keep = (sb(k, [P, 2, U, D]) for k in ("xr", "st", "ent", "keep"))
        stat, mv = sb("stat", [P, 2, U, 6]), sb("mv", [P, 2, U, 2])
        var, inv, root, shift = (sb(k, [P, 2, U]) for k in ("var", "inv", "root", "shift"))
        block = s.enter_context(nc.Block())
        K = 3 * U + 1

        @block.vector
        def _(dve):
            v = nc.vector

            def stats(i, h):
                ch = Marks(dve, links[h], i * K)
                gate(dve, loaded[h], (i + 1) * 16, dve_passed)
                gate(dve, gathered[h], (i + 1) * (16 * U), dve_passed)
                for u in range(U):
                    ch.mark(v.scalar_tensor_tensor(xr[:, h, u, :], st[:, h, u, :], g.root[:, bass.ds(i * (2 * U) + h * U + u, 1)],
                                                   xr[:, h, u, :], ALU.mult, ALU.add))
                gate(dve, links[h], i * K + U, dve_passed)
                row_stats(v, ch, dve_passed, stat[:, h], mv[:, h], var[:, h, :], xr[:, h], U, mv[:, h]).then_inc(varied[h], 1)

            def scale(i, h):
                ch = Marks(dve, links[h], i * K + 3 * U)
                dve.wait_ge(rooted[h], i + 1)
                ch.link(v.reciprocal(inv[:, h, :], root[:, h, :]))
                v.scalar_tensor_tensor(shift[:, h, :], mv[:, h, :, 0], -1.0, inv[:, h, :], ALU.mult, ALU.mult).then_inc(steadied[h], 1)

            def finish(turns_done, h):
                dve.wait_ge(normed[h], turns_done)
                v.scalar_tensor_tensor(keep[:, h], ent[:, h], 3.0, xr[:, h], ALU.mult, ALU.add).then_inc(finished[h], 1)

            with dve.Fori(0, STEPS) as i:
                stats(i, 0)
                scale(i, 0)
                with dve.If(i > 0):
                    finish(i, 1)
                stats(i, 1)
                scale(i, 1)
                dve.wait_ge(stored[0], i * 32)
                finish(i + 1, 0)
                gate(dve, stored[1], i * 32, dve_passed)
            finish(STEPS, 1)

        @block.scalar
        def _(act):
            with act.Fori(0, STEPS) as i:
                for h in range(2):
                    act.wait_ge(varied[h], i + 1)
                    nc.scalar.activation(root[:, h, :], var[:, h, :], ACT.Sqrt).then_inc(rooted[h], 1)
                    gate(act, stored[h], i * 32, act_passed)
                    act.wait_ge(steadied[h], i + 1)
                    for u in range(U):
                        last = nc.scalar.activation(ent[:, h, u, :], xr[:, h, u, :], ACT.Relu, bias=shift[:, h, u:u + 1],
                                                    scale=inv[:, h, u:u + 1])
                    last.then_inc(normed[h], 1)

        @block.sync
        def _(sp):
            def load(i, at, h):
                gate(sp, finished[h], i, sp_passed)
                sp.dma_start(xr[:, h], rows_of(x_rows, (at * (2 * U) + h * U) * P, U)).then_inc(loaded[h], 16)

            for h in range(2):
                load(0, 0, h)
            with sp.Fori(0, STEPS) as i:
                for h in range(2):
                    row = (i * (2 * U) + h * U) * P
                    load(i + 1, (i + 1) % STEPS, h)
                    gate(sp, normed[h], i + 1, sp_passed)
                    sp.dma_start(rows_of(entity_rows, row, U), ent[:, h]).then_inc(stored[h], 16)
                    gate(sp, finished[h], i + 1, sp_passed)
                    sp.dma_start(rows_of(kept, row, U), keep[:, h]).then_inc(stored[h], 16)
            for h in range(2):
                sp.wait_ge(loaded[h], (STEPS + 1) * 16)
                sp.wait_ge(stored[h], STEPS * 32)

        @block.gpsimd
        def _(pool):
            with pool.Fori(0, STEPS) as i:
                for h in range(2):
                    gate(pool, varied[h], i, passed)
                    nc.gpsimd.tensor_copy(index[:, h, :], g.state_index[:, bass.ds(i * (2 * U) + h * U, U)]).then_inc(copied, 1)
                    gate(pool, copied, i * 2 + h + 1, passed)
                    for u in range(U):
                        nc.gpsimd.indirect_dma_start(st[:, h, u, :], None, states,
                                                     bass.IndirectOffsetOnAxis(ap=index[:, h, u:u + 1], axis=0)).then_inc(gathered[h], 16)


def attention(nc, c, g, name, rec, att, source, index, own, own_index, emb, q_w, k_w, first_rows, messages, steps_of=None):
    packed = steps_of is not None
    with Phase(nc) as s:
        sem = lambda n: s.semaphore(f"{name}_{n}")
        passed, dve_passed, sp_passed, copied, first_stored, made, w_loaded = (
            sem(n) for n in ("passed", "dve_passed", "sp_passed", "copied", "first_stored", "made", "w_loaded"))
        (loaded, staged, mended, spread, marked, related, typed, turned, flipped, held, moved, keyed, asked, felt,
         scored, weighed, stored) = (
            halves(s, nc, f"{name}_{n}") for n in (
                "loaded", "staged", "mended", "spread", "marked", "related", "typed", "turned", "flipped", "held",
                "moved", "keyed", "asked", "felt", "scored", "weighed", "stored"))
        sb = lambda n, shape, dt=F32: s.enter_context(nc.sbuf_tensor(f"{name}_{n}", shape, dt))
        first_done, gathered = s.lasting(f"{name}_first_done"), lasting_halves(s, f"{name}_gathered")
        own_gathered = lasting_halves(s, f"{name}_own_gathered") if packed else None
        ix, ox, relation = sb("ix", [P, 2, V], I32), sb("ox", [P, 2, V], I32), sb("relation", [P, 2, V])

        def turns(engine, steps):
            with engine.Fori(0, TURNS) as i:
                if packed:
                    with engine.If(i < steps):
                        yield i
                else:
                    yield i

        firsts = sb("firsts", [TROWS, CHUNKS, D])
        wq, wk, emb_sb = sb("wq", [D, D]), sb("wk", [D, D]), sb("emb", [RELATIONS, D])
        own_sb, first_sb, got = sb("own", [P, 2, V, D]), sb("first", [P, 2, V, D]), sb("got", [P, 2, V, D])
        onehot = sb("onehot", [RELATIONS, 2, V, P])
        message, message_t, own_t = sb("message", [P, 2, V, D]), sb("message_t", [P, 2, V, P]), sb("own_t", [P, 2, V, P])
        right, product = sb("right", [P, 2, V, D]), sb("product", [P, 2, V, D])
        ps = {n: s.enter_context(nc.psum_tensor(f"{name}_ps_{n}", [P, V, P], F32))
              for n in ("types", "rel", "own_t", "message_t", "right", "left")}
        block = s.enter_context(nc.Block())

        @block.sync
        def _(sp):
            for a, b in ((wq, q_w), (wk, k_w), (emb_sb, emb)):
                sp.dma_start(a[:], b).then_inc(w_loaded, 16)
            steps = steps_of(sp) if packed else TURNS
            if not packed:
                sp.wait_ge(first_done, 16 * CHUNKS)
                sp.dma_start(first_rows.rearrange("(q r) d -> r q d", r=TROWS), firsts[:]).then_inc(first_stored, 16)
                sp.wait_ge(first_stored, 16)

            def load(i, at, h):
                t = at * (2 * V) + h * V
                gate(sp, held[h], i, sp_passed)
                sp.dma_start(own_sb[:, h], rows_of(own, t * P, V)).then_inc(loaded[h], 16)
                sp.dma_start(first_sb[:, h], first_rows[bass.ds(t, V), :].unsqueeze(0).broadcast_to([P, V, D])).then_inc(loaded[h], 16)

            if not packed:
                for h in range(2):
                    load(0, 0, h)
            for i in turns(sp, steps):
                for h in range(2):
                    gate(sp, related[h], i + 1, sp_passed)
                    sp.dma_start(rows_of(messages, (i * (2 * V) + h * V) * P, V), message[:, h]).then_inc(stored[h], 16)
                if not packed:
                    for h in range(2):
                        load(i + 1, (i + 1) % TURNS, h)
            for h in range(2):
                if not packed:
                    sp.wait_ge(loaded[h], (TURNS + 1) * 32)
                gate(sp, stored[h], steps * 16, sp_passed)

        @block.gpsimd
        def _(pool):
            steps = steps_of(pool) if packed else TURNS
            if not packed:
                for q in range(CHUNKS):
                    nc.gpsimd.indirect_dma_start(firsts[:, q, :], None, source,
                                                 bass.IndirectOffsetOnAxis(ap=own_index[:, q:q + 1], axis=0)).then_inc(first_done, 16)
            for i in turns(pool, steps):
                for h in range(2):
                    gate(pool, related[h], i, passed)
                    nc.gpsimd.tensor_copy(ix[:, h, :], index[:, bass.ds(i * (2 * V) + h * V, V)]).then_inc(copied, 1)
                    if packed:
                        gate(pool, held[h], i, passed)
                        nc.gpsimd.tensor_copy(ox[:, h, :], own_index[:, bass.ds(i * (2 * V) + h * V, V)]).then_inc(copied, 1)
                    gate(pool, copied, (i * 2 + h + 1) * (2 if packed else 1), passed)
                    for u in range(V):
                        nc.gpsimd.indirect_dma_start(got[:, h, u, :], None, source,
                                                     bass.IndirectOffsetOnAxis(ap=ix[:, h, u:u + 1], axis=0)).then_inc(gathered[h], 16)
                    if packed:
                        for u in range(V):
                            nc.gpsimd.indirect_dma_start(own_sb[:, h, u, :], None, own,
                                                         bass.IndirectOffsetOnAxis(ap=ox[:, h, u:u + 1], axis=0)).then_inc(own_gathered[h], 16)

        @block.vector
        def _(dve):
            v = nc.vector

            def stage(i, at, h):
                dve.wait_ge(spread[h], i)
                v.tensor_scalar(relation[:, h, :], rec[:, bass.ds(at * (2 * V) + h * V, V), 2], 0.0, None, ALU.add).then_inc(staged[h], 1)

            def mend(i, h):
                if packed:
                    return
                gate(dve, loaded[h], (i + 1) * 32, dve_passed)
                mask = g.in_first4[:, h, :]
                dve.wait_ge(held[h], i)
                v.tensor_scalar(mask, g.in_first[:, bass.ds(i * (2 * V) + h * V, V)], 0.0, None, ALU.add).then_inc(marked[h], 1)
                gate(dve, marked[h], i + 1, dve_passed)
                v.copy_predicated(own_sb[:, h], mask.unsqueeze(2).broadcast_to([P, V, D]), first_sb[:, h]).then_inc(mended[h], 1)

            def one_hot(i, h):
                dve.wait_ge(spread[h], i + 1)
                dve.wait_ge(typed[h], i)
                v.tensor_scalar(onehot[:, h], ps["types"][0:RELATIONS], c.part[0:RELATIONS, :], None, ALU.is_equal).then_inc(turned[h], 1)

            def relate(i, h):
                dve.wait_ge(typed[h], i + 1)
                dve.wait_ge(gathered[h], (i + 1) * (16 * V))
                dve.wait_ge(stored[h], i * 16)
                dve.wait_ge(flipped[h], i)
                v.tensor_tensor(message[:, h], ps["rel"][:], got[:, h], ALU.mult).then_inc(related[h], 1)

            def score(turns_done, h):
                dve.wait_ge(felt[h], turns_done)
                dve.wait_ge(asked[h], turns_done)
                v.tensor_tensor(product[:, h], ps["left"][:], right[:, h], ALU.mult).then_inc(scored[h], 1)
                dve.wait_ge(scored[h], turns_done)
                v.tensor_reduce(g.score4[:, h, :], product[:, h], axis=AX.X, op=ALU.add).then_inc(weighed[h], 1)
                dve.wait_ge(weighed[h], turns_done)
                column = within(nc, turns_done * (2 * V) - (2 - h) * V, TILES - V)
                v.tensor_scalar(att[:, bass.ds(column, V)], g.score4[:, h, :], 0.0, None, ALU.add)

            stage(0, 0, 0)
            stage(0, 0, 1)
            one_hot(0, 0)
            steps = steps_of(dve) if packed else TURNS
            for i in turns(dve, steps):
                relate(i, 0)
                mend(i, 0)
                stage(i + 1, (i + 1) % steps, 0)
                one_hot(i, 1)
                with dve.If(i > 0):
                    score(i, 1)
                relate(i, 1)
                mend(i, 1)
                stage(i + 1, (i + 1) % steps, 1)
                one_hot(i + 1, 0)
                score(i + 1, 0)
            score(steps, 1)

        @block.tensor
        def _(pe):
            def spread_types(i, h):
                pe.wait_ge(staged[h], i + 1)
                pe.wait_ge(turned[1 - h], i + h)
                for u in range(V):
                    last = nc.tensor.transpose(ps["types"][:, u, :], relation[:, h, u:u + 1].broadcast_to([P, P]),
                                               c.ident[:])
                last.then_inc(spread[h], 1)

            def look_up(i, h):
                pe.wait_ge(turned[h], i + 1)
                pe.wait_ge(related[1 - h], i + h)
                for u in range(V):
                    last = nc.tensor.matmul(ps["rel"][:, u, :], onehot[:, h, u, :], emb_sb[:], start=u == 0, stop=u == V - 1,
                                            skip_group_check=True)
                last.then_inc(typed[h], 1)

            pe.wait_ge(w_loaded, 48)
            spread_types(0, 0)
            look_up(0, 0)
            steps = steps_of(pe) if packed else TURNS
            for i in turns(pe, steps):
                for h in range(2):
                    spread_types(i + h, 1 - h)
                    pe.wait_ge(related[h], i + 1)
                    pe.wait_ge(keyed[1 - h], i + h)
                    for u in range(V):
                        last = nc.tensor.transpose(ps["message_t"][:, u, :], message[:, h, u, :], c.ident[:])
                    last.then_inc(flipped[h], 1)
                    if packed:
                        pe.wait_ge(own_gathered[h], (i + 1) * (16 * V))
                    else:
                        pe.wait_ge(mended[h], i + 1)
                    pe.wait_ge(moved[1 - h], i + h)
                    for u in range(V):
                        last = nc.tensor.transpose(ps["own_t"][:, u, :], own_sb[:, h, u, :], c.ident[:])
                    last.then_inc(held[h], 1)
                    look_up(i + h, 1 - h)
                    pe.wait_ge(keyed[h], i + 1)
                    pe.wait_ge(felt[1 - h], i + h)
                    for u in range(V):
                        last = nc.tensor.matmul(ps["right"][:, u, :], message_t[:, h, u, :], wk[:], start=u == 0, stop=u == V - 1,
                                                skip_group_check=True)
                    last.then_inc(made, 1)
                    pe.wait_ge(moved[h], i + 1)
                    pe.wait_ge(scored[1 - h], i + h)
                    for u in range(V):
                        last = nc.tensor.matmul(ps["left"][:, u, :], own_t[:, h, u, :], wq[:], start=u == 0, stop=u == V - 1,
                                                skip_group_check=True)
                    last.then_inc(asked[h], 1)

        @block.scalar
        def _(act):
            steps = steps_of(act) if packed else TURNS
            for i in turns(act, steps):
                for h in range(2):
                    act.wait_ge(flipped[h], i + 1)
                    nc.scalar.activation(message_t[:, h], ps["message_t"][:], ACT.Copy).then_inc(keyed[h], 1)
                    act.wait_ge(held[h], i + 1)
                    nc.scalar.activation(own_t[:, h], ps["own_t"][:], ACT.Copy).then_inc(moved[h], 1)
                    act.wait_ge(scored[h], i)
                    act.wait_ge(made, i * 2 + h + 1)
                    nc.scalar.activation(right[:, h], ps["right"][:], ACT.Tanh).then_inc(felt[h], 1)


def softmax_weights(nc, c, g, name, att, weight, scratch):
    segment_reduce(nc, c, g, f"{name}max", att, g.top, ALU.max)
    packed = isinstance(g, LiveEdges)
    if packed:
        simple(nc, f"{name}dead", [
            lambda v: v.tensor_scalar(scratch[:], g.dead[:], 0.0, None, ALU.is_gt),
            lambda v: v.tensor_scalar(scratch[:], scratch[:], LIMIT, -LIMIT, ALU.mult, ALU.add),
            lambda v: v.tensor_tensor(g.top[:], g.top[:], scratch[:], ALU.max),
            lambda v: v.tensor_scalar(scratch[:], g.top[:], 0.0, None, ALU.max),
            None,
            lambda v: v.tensor_tensor(g.extra[:], scratch[:], g.dead[:], ALU.mult),
        ], lambda act: act.activation(scratch[:], scratch[:], ACT.Exp, scale=-1.0))
    with Phase(nc) as s:
        below, raised = s.semaphore(f"{name}_below"), s.semaphore(f"{name}_raised")
        block = s.enter_context(nc.Block())

        @block.vector
        def _(dve):
            nc.vector.tensor_tensor(weight[:], att[:], g.top[:], ALU.subtract).then_inc(below, 1)

        @block.scalar
        def _(act):
            act.wait_ge(below, 1)
            nc.scalar.activation(weight[:], weight[:], ACT.Exp).then_inc(raised, 1)

    segment_reduce(nc, c, g, f"{name}sum", weight, g.top, ALU.add)
    if packed:
        simple(nc, f"{name}all", [lambda v: v.tensor_tensor(g.top[:], g.top[:], g.extra[:], ALU.add)])
    with Phase(nc) as s:
        chain = s.semaphore(f"{name}_scaled")
        block = s.enter_context(nc.Block())

        @block.vector
        def _(dve):
            ch = Chain(dve, chain)
            ch.link(nc.vector.tensor_tensor(g.top[:], g.top[:], g.count[:], ALU.mult))
            ch.link(nc.vector.reciprocal(g.scale[:], g.top[:]))


def aggregate(nc, c, g, name, weight, messages, target):
    with Phase(nc) as s:
        sem = lambda n: s.semaphore(f"{name}_{n}")
        sp_passed, act_passed, dve_passed, opened = (sem(n) for n in ("sp_passed", "act_passed", "dve_passed", "opened"))
        staged, spread, matched, summed, handed, completed, evacuated, rooted, ranged, blended, loaded, stored = (
            halves(s, nc, f"{name}_{n}") for n in ("staged", "spread", "matched", "summed", "handed", "completed", "evacuated",
                                                   "rooted", "ranged", "blended", "loaded", "stored"))
        act_squared, inverted = halves(s, nc, f"{name}_squared"), halves(s, nc, f"{name}_inverted")
        sb = lambda n, shape, dt=F32: s.enter_context(nc.sbuf_tensor(f"{name}_{n}", shape, dt))
        cols, got = sb("cols", [P, 2, U + 1]), sb("got", [P, 2, U, D])
        same, into = sb("same", [P, 2, U, P]), sb("into", [1, 2, U, P])
        carry = sb("carry", [1, 2, U, D])
        new, fresh, junk = (sb(k, [P, 2, U, D]) for k in ("new", "fresh", "junk"))
        square, length = sb("square", [P, 2, U]), sb("length", [P, 2, U])
        src_ps = s.enter_context(nc.psum_tensor(f"{name}_src", [P, 8, P], F32))
        sum_ps = [s.enter_context(nc.psum_tensor(f"{name}_sum{h}", [P, 8, P], F32)) for h in range(2)]
        block = s.enter_context(nc.Block())

        packed = isinstance(g, LiveEdges)

        def column(steps, j, h):
            return within(nc, steps * (2 * U) - U - j * (2 * U) - h * U, TILES - U)

        def turns(engine):
            steps = live_steps(engine, g) if packed else STEPS
            with engine.Fori(0, STEPS) as n:
                if packed:
                    with engine.If(n < steps):
                        yield steps, n
                else:
                    yield steps, n

        def behind(h, u):
            return carry[:, h, u + 1, :] if u < U - 1 else carry[:, 1 - h, 0, :]

        @block.vector
        def _(dve):
            v = nc.vector

            def stage(col, n, h):
                dve.wait_ge(spread[h], n)
                v.tensor_scalar(cols[:, h, :], g.src[:, bass.ds(col, U + 1)], 0.0, None, ALU.add).then_inc(staged[h], 1)

            def match(col, n, h):
                dve.wait_ge(staged[h], n + 1)
                dve.wait_ge(spread[h], n + 1)
                dve.wait_ge(completed[h], n)
                for u in range(U):
                    v.tensor_scalar(same[:, h, u, :], src_ps[:, u, :], g.src[:, bass.ds(col + u, 1)],
                                    weight[:, bass.ds(col + u, 1)], ALU.is_equal, ALU.mult)
                v.tensor_tensor(into[:, h], src_ps[0:1, 0:U, :], cols[0:1, h, 1:U + 1].unsqueeze(2).broadcast_to([1, U, P]),
                                ALU.is_equal).then_inc(matched[h], 1)

            def chain(col, n, h):
                dve.wait_ge(summed[h], n + 1)
                dve.wait_ge(completed[1 - h], n + h)
                for u in reversed(range(U)):
                    v.scalar_tensor_tensor(carry[:, h, u, :], behind(h, u), g.whole_next[0:1, bass.ds(col + u, 1)],
                                           sum_ps[h][0:1, u, :], ALU.mult, ALU.add).then_inc(handed[h], 1)
                    dve.wait_ge(handed[h], n * U + (U - u))

            def finish(turns_done, h):
                dve.wait_ge(rooted[h], turns_done)
                v.tensor_scalar(length[:, h, :], length[:, h, :], 1e-12, None, ALU.max).then_inc(ranged[h], 1)
                dve.wait_ge(ranged[h], turns_done)
                v.reciprocal(length[:, h, :], length[:, h, :]).then_inc(inverted[h], 1)
                dve.wait_ge(inverted[h], turns_done)
                v.tensor_tensor(new[:, h], fresh[:, h], length[:, h, :].unsqueeze(2).broadcast_to([P, U, D]),
                                ALU.mult).then_inc(blended[h], 1)

            v.memset(carry[:], 0.0).then_inc(opened, 1)
            dve.wait_ge(opened, 1)
            steps = live_steps(dve, g) if packed else STEPS
            stage(column(steps, 0, 0), 0, 0)
            match(column(steps, 0, 0), 0, 0)
            for steps, n in turns(dve):
                for h in range(2):
                    following = column(steps, (n + h) % steps, 1 - h)
                    stage(following, n + h, 1 - h)
                    chain(column(steps, n, h), n, h)
                    match(following, n + h, 1 - h)
                    if h == 0:
                        with dve.If(n > 0):
                            finish(n, 1)
                    else:
                        dve.wait_ge(stored[0], n * 16)
                        finish(n + 1, 0)
                gate(dve, stored[1], n * 16, dve_passed)
            finish(steps, 1)

        @block.tensor
        def _(pe):
            def spread_sources(n, h):
                pe.wait_ge(staged[h], n + 1)
                pe.wait_ge(matched[1 - h], n + h)
                for u in range(U):
                    last = nc.tensor.transpose(src_ps[:, u, :], cols[:, h, u:u + 1].broadcast_to([P, P]), c.ident[:])
                last.then_inc(spread[h], 1)

            spread_sources(0, 0)
            for steps, n in turns(pe):
                for h in range(2):
                    pe.wait_ge(matched[h], n + 1)
                    pe.wait_ge(loaded[h], (n + 1) * 16)
                    pe.wait_ge(evacuated[h], n)
                    for u in range(U):
                        last = nc.tensor.matmul(sum_ps[h][:, u, :], same[:, h, u, :], got[:, h, u, :],
                                                start=u % 4 == 0, stop=False, skip_group_check=True)
                    last.then_inc(summed[h], 1)
                    spread_sources(n + h, 1 - h)
                    pe.wait_ge(handed[h], (n + 1) * U)
                    for u in range(U):
                        last = nc.tensor.matmul(sum_ps[h][:, u, :], into[:, h, u, :], behind(h, u), start=False,
                                                stop=u in (3, U - 1), skip_group_check=True)
                    last.then_inc(completed[h], 1)

        @block.scalar
        def _(act):
            for steps, n in turns(act):
                for h in range(2):
                    gate(act, blended[h], n, act_passed)
                    gate(act, completed[h], n + 1, act_passed)
                    for u in range(U):
                        last = nc.scalar.activation(fresh[:, h, u, :], sum_ps[h][:, u, :], ACT.Copy,
                                                    scale=g.scale[:, bass.ds(column(steps, n, h) + u, 1)])
                    last.then_inc(evacuated[h], 1)
                    act.wait_ge(evacuated[h], n + 1)
                    for u in range(U):
                        last = nc.scalar.activation(junk[:, h, u, :], fresh[:, h, u, :], ACT.Square, accum_out=square[:, h, u:u + 1])
                    last.then_inc(act_squared[h], 1)
                    act.wait_ge(act_squared[h], n + 1)
                    nc.scalar.activation(length[:, h, :], square[:, h, :], ACT.Sqrt).then_inc(rooted[h], 1)

        @block.sync
        def _(sp):
            steps = live_steps(sp, g) if packed else STEPS
            for h in range(2):
                sp.dma_start(got[:, h], rows_of(messages, column(steps, 0, h) * P, U)).then_inc(loaded[h], 16)
            for steps, n in turns(sp):
                for h in range(2):
                    gate(sp, summed[h], n + 1, sp_passed)
                    sp.dma_start(got[:, h], rows_of(messages, column(steps, (n + 1) % steps, h) * P, U)).then_inc(loaded[h], 16)
                for h in range(2):
                    gate(sp, blended[h], n + 1, sp_passed)
                    sp.dma_start(rows_of(target, column(steps, n, h) * P, U), new[:, h]).then_inc(stored[h], 16)
            for h in range(2):
                gate(sp, loaded[h], (steps + 1) * 16, sp_passed)
                gate(sp, stored[h], steps * 16, sp_passed)


def final_rows(nc, c, g, kept, parts, totals, out):
    with Phase(nc) as s:
        sem = lambda n: s.semaphore(f"o_{n}")
        passed, sp_passed, copied = (sem(n) for n in ("passed", "sp_passed", "copied"))
        loaded, added, stored = (halves(s, nc, f"o_{n}") for n in ("loaded", "added", "stored"))
        sent = lasting_halves(s, "o_sent")
        sb = lambda n, shape, dt=F32: s.enter_context(nc.sbuf_tensor(f"o_{n}", shape, dt))
        index = sb("index", [P, 2, U], I32)
        rows = sb("rows", [P, 2, 2, U, D])
        block = s.enter_context(nc.Block())

        @block.sync
        def _(sp):
            def load(i, at, h):
                gate(sp, sent[h], i * (16 * U), sp_passed)
                gate(sp, stored[h], i * 16, sp_passed)
                for k, table in enumerate([kept] + parts):
                    sp.dma_start(rows[:, k, h], rows_of(table, (at * (2 * U) + h * U) * P, U)).then_inc(loaded[h], 16)

            for h in range(2):
                load(0, 0, h)
            with sp.Fori(0, STEPS) as i:
                for h in range(2):
                    gate(sp, added[h], i + 1, sp_passed)
                    sp.dma_start(rows_of(totals, (i * (2 * U) + h * U) * P, U), rows[:, 0, h]).then_inc(stored[h], 16)
                    load(i + 1, (i + 1) % STEPS, h)
            for h in range(2):
                sp.wait_ge(loaded[h], (STEPS + 1) * 32)
                sp.wait_ge(stored[h], STEPS * 16)

        @block.vector
        def _(dve):
            with dve.Fori(0, STEPS) as i:
                for h in range(2):
                    dve.wait_ge(loaded[h], (i + 1) * 32)
                    nc.vector.tensor_tensor(rows[:, 0, h], rows[:, 0, h], rows[:, 1, h], ALU.add).then_inc(added[h], 1)

        @block.gpsimd
        def _(pool):
            with pool.Fori(0, STEPS) as i:
                for h in range(2):
                    gate(pool, sent[h], i * (16 * U), passed)
                    nc.gpsimd.tensor_copy(index[:, h, :], g.out_index[:, bass.ds(i * (2 * U) + h * U, U)]).then_inc(copied, 1)
                    gate(pool, copied, i * 2 + h + 1, passed)
                    gate(pool, added[h], i + 1, passed)
                    for u in range(U):
                        nc.gpsimd.indirect_dma_start(out, bass.IndirectOffsetOnAxis(ap=index[:, h, u:u + 1], axis=0),
                                                     rows[:, 0, h, u, :], None, bounds_check=NODES - 1,
                                                     oob_is_err=False).then_inc(sent[h], 16)
            for h in range(2):
                pool.wait_ge(sent[h], STEPS * (16 * U))


def add_live_rows(nc, c, g, totals, parts, out):
    with Phase(nc) as s:
        sem = lambda n: s.semaphore(f"l_{n}")
        passed, sp_passed, copied = (sem(n) for n in ("passed", "sp_passed", "copied"))
        loaded, added = (halves(s, nc, f"l_{n}") for n in ("loaded", "added"))
        sent = lasting_halves(s, "l_sent")
        sb = lambda n, shape, dt=F32: s.enter_context(nc.sbuf_tensor(f"l_{n}", shape, dt))
        gathered, links = lasting_halves(s, "l_gathered"), halves(s, nc, "l_links")
        index, whence = sb("index", [P, 2, U], I32), sb("whence", [P, 2, U], I32)
        rows, total = sb("rows", [P, 2, 2, U, D]), sb("total", [P, 2, U, D])
        block = s.enter_context(nc.Block())

        def turns(engine):
            steps = live_steps(engine, g)
            with engine.Fori(0, STEPS) as i:
                with engine.If(i < steps):
                    yield i

        @block.sync
        def _(sp):
            for i in turns(sp):
                for h in range(2):
                    gate(sp, sent[h], i * (16 * U), sp_passed)
                    for k, table in enumerate(parts):
                        sp.dma_start(rows[:, k, h], rows_of(table, (i * (2 * U) + h * U) * P, U)).then_inc(loaded[h], 16)

        @block.vector
        def _(dve):
            for i in turns(dve):
                for h in range(2):
                    dve.wait_ge(loaded[h], (i + 1) * 32)
                    nc.vector.tensor_tensor(rows[:, 0, h], rows[:, 0, h], rows[:, 1, h], ALU.add).then_inc(links[h], 1)
                    dve.wait_ge(links[h], i + 1)
                    dve.wait_ge(gathered[h], (i + 1) * (16 * U))
                    nc.vector.tensor_tensor(rows[:, 0, h], rows[:, 0, h], total[:, h], ALU.add).then_inc(added[h], 1)

        @block.gpsimd
        def _(pool):
            for i in turns(pool):
                for h in range(2):
                    gate(pool, sent[h], i * (16 * U), passed)
                    nc.gpsimd.tensor_copy(index[:, h, :], g.out_index[:, bass.ds(i * (2 * U) + h * U, U)]).then_inc(copied, 1)
                    nc.gpsimd.tensor_copy(whence[:, h, :], g.columns["src_first"][:, bass.ds(i * (2 * U) + h * U, U)]).then_inc(copied, 1)
                    gate(pool, copied, i * 4 + 2 * h + 2, passed)
                    for u in range(U):
                        nc.gpsimd.indirect_dma_start(total[:, h, u, :], None, totals,
                                                     bass.IndirectOffsetOnAxis(ap=whence[:, h, u:u + 1], axis=0)).then_inc(gathered[h], 16)
                for h in range(2):
                    gate(pool, added[h], i + 1, passed)
                    for u in range(U):
                        nc.gpsimd.indirect_dma_start(out, bass.IndirectOffsetOnAxis(ap=index[:, h, u:u + 1], axis=0),
                                                     rows[:, 0, h, u, :], None, bounds_check=NODES - 1,
                                                     oob_is_err=False).then_inc(sent[h], 16)
            steps = live_steps(pool, g)
            for h in range(2):
                gate(pool, sent[h], steps * (16 * U), passed)


def rank_live(nc, c, g, live):
    with Phase(nc) as s:
        chain, asked, counted = (s.semaphore(f"r_{n}") for n in ("chain", "asked", "counted"))
        sb = lambda n, shape, dt=F32: s.enter_context(nc.sbuf_tensor(f"r_{n}", shape, dt))
        total, running, zero = sb("total", [P, TILES]), sb("running", [P, TILES]), sb("zero", [P, TILES])
        marks, full = sb("marks", [1, TURNS]), sb("full", [1, TURNS])
        amount, last_row = sb("amount", [1, 2]), sb("last_row", [P, 1])
        ps_in, ps_all = (s.enter_context(nc.psum_tensor(f"r_ps{i}", [P, 512], F32)) for i in range(2))
        block = s.enter_context(nc.Block())

        @block.tensor
        def _(pe):
            nc.tensor.matmul(ps_in[:, 0:TILES], c.tri[:], g.live[:], start=True, stop=True)
            nc.tensor.matmul(ps_all[:, 0:TILES], c.ones[:], g.live[:], start=True, stop=True).then_inc(counted, 1)

        @block.gpsimd
        def _(pool):
            pool.iota(marks[:], pattern=[[1, TURNS]], base=0, channel_multiplier=0,
                      allow_small_or_imprecise_dtypes=True).then_inc(asked, 1)

        @block.vector
        def _(dve):
            v, ch = nc.vector, Chain(dve, chain)
            ch.link(v.memset(zero[:], 0.0))
            dve.wait_ge(counted, 1)
            ch.link(v.tensor_copy(total[:], ps_all[:, 0:TILES]))
            ch.link(v.tensor_tensor_scan(running[:], total[:], zero[:], 0.0, ALU.add, ALU.add))
            ch.link(v.tensor_scalar(last_row[:], running[:, TILES - 1:TILES], -1.0, 0.0, ALU.add, ALU.max))
            ch.link(v.tensor_tensor(total[:], running[:], total[:], ALU.subtract))
            ch.link(v.tensor_tensor(g.before[:], ps_in[:, 0:TILES], total[:], ALU.add))
            ch.link(v.tensor_scalar(g.before_capped[:], g.before[:], last_row[:], None, ALU.min))
            dve.wait_ge(asked, 1)
            for out, tiles, n in ((live.steps, 2 * U, STEPS), (live.turns, 2 * V, TURNS)):
                ch.link(v.tensor_scalar(full[:, 0:n], marks[:, 0:n], float(tiles * P), running[0:1, TILES - 1:TILES],
                                        ALU.mult, ALU.is_lt))
                ch.link(v.tensor_reduce(amount[:, 0:1], full[:, 0:n], axis=AX.X, op=ALU.add))
                ch.link(v.tensor_scalar(out[:], amount[:, 0:1], 1.0, None, ALU.max))


def row_address(nc, name, place, out, extra=None):
    with Phase(nc) as s:
        chain = s.semaphore(f"{name}_chain")
        a, b = (s.enter_context(nc.sbuf_tensor(f"{name}_{n}", [P, TILES], I32)) for n in "ab")
        block = s.enter_context(nc.Block())

        @block.vector
        def _(dve):
            v, ch = nc.vector, Chain(dve, chain)
            ch.link(v.tensor_copy(out[:], place[:]))
            ch.link(v.tensor_scalar(a[:], out[:], P - 1, None, ALU.bitwise_and))
            ch.link(v.tensor_scalar(b[:], out[:], 7, None, ALU.logical_shift_right))
            ch.link(v.scalar_tensor_tensor(out[:], a[:], float(TILES), b[:], ALU.mult, ALU.add))


def whole_table(nc, name, table, tile):
    with Phase(nc) as s:
        stored = s.semaphore(f"{name}_stored")
        block = s.enter_context(nc.Block())

        @block.sync
        def _(sp):
            sp.dma_start(table.rearrange("(p t) w -> p (t w)", t=TILES), tile[:].rearrange("p t w -> p (t w)")).then_inc(stored, 16)
            sp.wait_ge(stored, 16)


def pack_live(nc, c, g, live, records, index, table):
    with Phase(nc) as s:
        sem = lambda n: s.semaphore(f"k_{n}")
        passed, copied, loaded = sem("passed"), sem("copied"), sem("loaded")
        sent, staged = lasting_halves(s, "k_sent"), halves(s, nc, "k_staged")
        ix = s.enter_context(nc.sbuf_tensor("k_ix", [P, 2, U], I32))
        row = s.enter_context(nc.sbuf_tensor("k_row", [P, 2, U, LIVE_REC], I32))
        block = s.enter_context(nc.Block())

        @block.vector
        def _(dve):
            with dve.Fori(0, STEPS) as i:
                for h in range(2):
                    t = i * (2 * U) + h * U
                    dve.wait_ge(sent[h], i * (16 * U))
                    nc.vector.tensor_scalar(ix[:, h, :], index[:, bass.ds(t, U)], 0.0, None, ALU.add)
                    nc.vector.tensor_scalar(row[:, h], records[:, bass.ds(t, U), :], 0.0, None, ALU.add).then_inc(staged[h], 1)

        @block.gpsimd
        def _(pool):
            with pool.Fori(0, STEPS) as i:
                for h in range(2):
                    gate(pool, staged[h], i + 1, passed)
                    for u in range(U):
                        nc.gpsimd.indirect_dma_start(table, bass.IndirectOffsetOnAxis(ap=ix[:, h, u:u + 1], axis=0),
                                                     row[:, h, u, :], None, bounds_check=ROWS - 1, oob_is_err=False).then_inc(sent[h], 16)
            for h in range(2):
                pool.wait_ge(sent[h], STEPS * (16 * U))

    with Phase(nc) as s:
        loaded = s.semaphore("k_loaded")
        block = s.enter_context(nc.Block())

        @block.sync
        def _(sp):
            sp.dma_start(live.rec[:].rearrange("p t w -> p (t w)"), table.rearrange("(p t) w -> p (t w)", t=TILES)).then_inc(loaded, 16)
            sp.wait_ge(loaded, 16)


def look_up_live(nc, c, live, node_rows, g0_rows, live_g0, found):
    with Phase(nc) as s:
        sem = lambda n: s.semaphore(f"u_{n}")
        passed, sp_passed, copied = sem("passed"), sem("sp_passed"), sem("copied")
        taken, stored = halves(s, nc, "u_taken"), halves(s, nc, "u_stored")
        gathered = lasting_halves(s, "u_gathered")
        sb = lambda n, shape, dt=F32: s.enter_context(nc.sbuf_tensor(f"u_{n}", shape, dt))
        ia, ib = sb("ia", [P, 2, U], I32), sb("ib", [P, 2, U], I32)
        pair, rows = sb("pair", [P, 2, U, 2], I32), sb("rows", [P, 2, U, D])
        block = s.enter_context(nc.Block())

        def turns(engine):
            steps = live_steps(engine, live)
            with engine.Fori(0, STEPS) as i:
                with engine.If(i < steps):
                    yield i

        @block.gpsimd
        def _(pool):
            for i in turns(pool):
                for h in range(2):
                    t = i * (2 * U) + h * U
                    gate(pool, taken[h], i, passed)
                    gate(pool, stored[h], i * 16, passed)
                    nc.gpsimd.tensor_copy(ia[:, h, :], live.columns["table_index"][:, bass.ds(t, U)]).then_inc(copied, 1)
                    nc.gpsimd.tensor_copy(ib[:, h, :], live.columns["src_first"][:, bass.ds(t, U)]).then_inc(copied, 1)
                    gate(pool, copied, i * 4 + 2 * h + 2, passed)
                    for u in range(U):
                        nc.gpsimd.indirect_dma_start(pair[:, h, u, :], None, node_rows,
                                                     bass.IndirectOffsetOnAxis(ap=ia[:, h, u:u + 1], axis=0)).then_inc(gathered[h], 16)
                        nc.gpsimd.indirect_dma_start(rows[:, h, u, :], None, g0_rows,
                                                     bass.IndirectOffsetOnAxis(ap=ib[:, h, u:u + 1], axis=0)).then_inc(gathered[h], 16)

        @block.vector
        def _(dve):
            v = nc.vector
            for i in turns(dve):
                for h in range(2):
                    dve.wait_ge(gathered[h], (i + 1) * (32 * U))
                    v.tensor_scalar(found[:, bass.ds(i * (2 * U) + h * U, U), :], pair[:, h], 0.0, None, ALU.add).then_inc(taken[h], 1)

        @block.sync
        def _(sp):
            for i in turns(sp):
                for h in range(2):
                    gate(sp, gathered[h], (i + 1) * (32 * U), sp_passed)
                    sp.dma_start(rows_of(live_g0, (i * (2 * U) + h * U) * P, U), rows[:, h]).then_inc(stored[h], 16)
            steps = live_steps(sp, live)
            for h in range(2):
                gate(sp, stored[h], steps * 16, sp_passed)


def find_live(nc, c, g, live, tmp, records_dram, node_rows, g0_rows, live_g0, records, pairs):
    a, b, d, e = tmp
    rank_live(nc, c, g, live)
    segment_reduce(nc, c, g, "has_live", g.live, g.has_live, ALU.max)
    simple(nc, "k0", [lambda v: v.tensor_scalar(a[:], g.like[:], -1.0, 1.0, ALU.mult, ALU.add),
                      lambda v: v.tensor_tensor(a[:], a[:], g.place[:], ALU.mult)])
    segment_reduce(nc, c, g, "first_place", a, g.first, ALU.max)
    segment_reduce(nc, c, g, "degree", g.count, d, ALU.max)
    simple(nc, "k7", [lambda v: v.tensor_scalar(a[:], g.like[:], -1.0, 1.0, ALU.mult, ALU.add),
                      lambda v: v.tensor_tensor(a[:], a[:], g.before_capped[:], ALU.mult)])
    segment_reduce(nc, c, g, "first_live", a, e, ALU.max)
    row_address(nc, "k1", g.before, live.columns["state_a"])
    simple(nc, "k2", [
        lambda v: v.tensor_copy(pairs[:, :, 0], e[:]),
        lambda v: v.tensor_copy(pairs[:, :, 1], g.has_live[:]),
        lambda v: v.tensor_scalar(a[:], e[:], float(ROWS), None, ALU.add),
        lambda v: v.tensor_scalar(b[:], g.place[:], float(2 * ROWS), None, ALU.add),
        lambda v: v.tensor_tensor(a[:], a[:], b[:], ALU.subtract),
        lambda v: v.tensor_tensor(a[:], a[:], g.has_live[:], ALU.mult),
        lambda v: v.tensor_tensor(a[:], a[:], b[:], ALU.add),
        lambda v: v.tensor_copy(g.state_index[:], a[:]),
        lambda v: v.tensor_scalar(b[:], g.live[:], -float(FAR), float(FAR), ALU.mult, ALU.add),
        lambda v: v.tensor_tensor(live.columns["state_b"][:], live.columns["state_a"][:], b[:], ALU.add),
        lambda v: v.memset(live.rec[:], 0),
        lambda v: v.memset(live.rec[:, :, 0], NODES),
        lambda v: v.memset(live.rec[:, :, 4], 1),
        lambda v: v.memset(records[:], 0),
        lambda v: v.tensor_copy(records[:, :, 0], g.src[:, 0:TILES]),
        lambda v: v.tensor_copy(records[:, :, 1], g.dst_first[:]),
        lambda v: v.tensor_copy(records[:, :, 2], c.rec[:, :, 2]),
        lambda v: v.tensor_copy(records[:, :, 3], g.place[:]),
        lambda v: v.tensor_copy(records[:, :, 4], d[:]),
        lambda v: v.tensor_copy(records[:, :, 5], g.first[:]),
    ])
    whole_table(nc, "k3", node_rows, pairs)
    whole_table(nc, "k4", records_dram, live.rec)
    pack_live(nc, c, g, live, records, live.columns["state_b"], records_dram)
    find_segments(nc, c, live, "lf", live.rec)
    row_address(nc, "k5", live.rec[:, :, 1], live.columns["table_index"])
    simple(nc, "k6", [
        lambda v: v.tensor_copy(live.columns["dst_first"][:], live.rec[:, :, 1]),
        lambda v: v.tensor_copy(live.columns["src_first"][:], live.rec[:, :, 5]),
        lambda v: v.tensor_copy(live.count[:], live.rec[:, :, 4]),
        lambda v: v.reciprocal(live.coef[:], live.count[:]),
        lambda v: v.tensor_scalar(live.coef[:], live.coef[:], 0.9, None, ALU.mult),
        lambda v: v.memset(a[:], 1.0),
        lambda v: v.memset(pairs[:], 0),
    ])
    segment_reduce(nc, c, live, "live_own", a, b, ALU.add)
    segment_reduce(nc, c, live, "live_all", b, d, ALU.max)
    simple(nc, "k7", [
        lambda v: v.tensor_tensor(live.dead[:], live.count[:], d[:], ALU.subtract),
        lambda v: v.tensor_scalar(live.dead[:], live.dead[:], 0.0, None, ALU.max),
        lambda v: v.tensor_scalar(a[:], live.like[:], -1.0, 1.0, ALU.mult, ALU.add),
        lambda v: v.tensor_tensor(a[:], a[:], g.place[:], ALU.mult)])
    segment_reduce(nc, c, live, "live_first", a, b, ALU.max)
    look_up_live(nc, c, live, node_rows, g0_rows, live_g0, pairs)
    cols = live.columns
    simple(nc, "k8", [
        lambda v: v.tensor_copy(cols["own_part"][:], b[:]),
        lambda v: v.tensor_copy(e[:], pairs[:, :, 1]),
        lambda v: v.tensor_scalar(b[:], cols["dst_first"][:], float(2 * ROWS), None, ALU.add),
        lambda v: v.tensor_copy(a[:], pairs[:, :, 0]),
        lambda v: v.tensor_tensor(d[:], a[:], b[:], ALU.subtract),
        lambda v: v.tensor_tensor(d[:], d[:], e[:], ALU.mult),
        lambda v: v.tensor_tensor(cols["state_a"][:], d[:], b[:], ALU.add),
        lambda v: v.tensor_scalar(b[:], e[:], float(ROWS), None, ALU.mult),
        lambda v: v.tensor_tensor(cols["state_b"][:], cols["state_a"][:], b[:], ALU.add),
        lambda v: v.tensor_scalar(a[:], a[:], -float(ZERO), None, ALU.add),
        lambda v: v.tensor_tensor(a[:], a[:], e[:], ALU.mult),
        lambda v: v.tensor_scalar(cols["target_part"][:], a[:], float(ZERO), None, ALU.add),
    ])


def live_turns(engine, live):
    return engine.value_load(live.turns[0:1, 0:1], min_val=1, max_val=TURNS)


def build(nc, x, src, dst, relation, emb, q_w, k_w, out):
    dram = lambda n, rows, cols=D, dt=F32: nc.dram_tensor(n, (rows, cols), dt, kind="Internal").ap()
    table = dram("table", TABLE, 2, I32)
    half_sorted, sorted_rows = dram("half_sorted", ROWS, REC, I32), dram("sorted_rows", ROWS, REC, I32)
    live_rows, node_rows = dram("live_rows", ROWS, LIVE_REC, I32), dram("node_rows", ROWS, 2, I32)
    x_rows, kept, messages, g0_rows, live_g0, totals = (dram(n, ROWS) for n in (
        "x_rows", "kept", "messages", "g0_rows", "live_g0", "totals"))
    states = dram("states", 3 * ROWS)
    entity = dram("entity", NODES + ROWS)
    parts = [dram(f"part{k}", ROWS + 1) for k in range(3)]
    first_rows = dram("first_rows", TILES)
    with ExitStack() as s:
        c = Persistent(nc, s)
        partial = [states[0:ROWS, :], states[ROWS:2 * ROWS, :], parts[1]]
        filled = nc.alloc_semaphore("filled")
        constants(nc, c)
        histogram(nc, c, src, dst, relation)
        node_table(nc, c, table)
        with nc.sbuf_tensor("zero", [P, 2 * U * D], F32) as zero:
            sort_pass(nc, c, "a", c.lo, LO, c.off_lo, half_sorted, Zeros(zero, partial, filled))
        reload(nc, c, "ra", half_sorted)
        sort_pass(nc, c, "b", c.hi, HI, c.off_hi, sorted_rows)
        reload(nc, c, "rb", sorted_rows)
        g = FullEdges(nc, s)
        find_segments(nc, c, g, "ff", c.rec)
        sb = lambda n, shape, dt=F32: s.enter_context(nc.sbuf_tensor(n, shape, dt))
        tmp = [sb(f"tmp{k}", [P, TILES]) for k in range(4)]
        att, weight, scratch = tmp[0], tmp[1], tmp[2]
        simple(nc, "ones", [lambda v: v.memset(weight[:], 1.0),
                            lambda v: v.tensor_scalar(g.x_index[:], c.rec[:, :, 0], float(NODES - 1), None, ALU.min)])
        number_places(nc, g)
        segment_reduce(nc, c, g, "count", weight, g.count, ALU.add)
        simple(nc, "roots", [None, lambda v: v.reciprocal(g.inv_root[:], g.root[:])],
               lambda act: act.activation(g.root[:], g.count[:], ACT.Sqrt))
        zero_rows(nc, parts[0:2])
        edge_info(nc, c, g, x, table, sorted_rows, x_rows, g0_rows, states, entity, out)
        live = LiveEdges(nc, s)
        with ExitStack() as inner:
            records = inner.enter_context(nc.sbuf_tensor("records", [P, TILES, LIVE_REC], I32))
            pairs = inner.enter_context(nc.sbuf_tensor("pairs", [P, TILES, 2], I32))
            find_live(nc, c, g, live, tmp, live_rows, node_rows, g0_rows, live_g0, records, pairs)
        propagate(nc, c, live, "p", g0_rows, states, live_g0, 10)
        own = entity[NODES:NODES + ROWS, :]
        second_norm(nc, c, g, x_rows, states, own, kept)
        attention(nc, c, g, "a0", c.rec, att, entity, g.entity_index, own, g.first_entity, emb, q_w, k_w, first_rows, messages)
        softmax_weights(nc, c, g, "w0", att, weight, scratch)
        aggregate(nc, c, g, "g0", weight, messages, parts[0])
        final_rows(nc, c, g, kept, parts[0:1], totals, out)
        cols = live.columns
        simple(nc, "clear_att", [lambda v: v.memset(att[:], 0.0)])
        for k, index, own_index in ((1, "dst_first", "src_first"), (2, "target_part", "own_part")):
            attention(nc, c, live, f"a{k}", live.rec, att, parts[k - 1], cols[index], parts[k - 1], cols[own_index], emb, q_w, k_w,
                      first_rows, messages, steps_of=lambda engine: live_turns(engine, live))
            softmax_weights(nc, c, live, f"w{k}", att, weight, scratch)
            aggregate(nc, c, live, f"g{k}", weight, messages, parts[k])
        add_live_rows(nc, c, live, totals, parts[1:3], out)


def number_places(nc, g):
    with Phase(nc) as s:
        block = s.enter_context(nc.Block())
        done = s.semaphore("place_done")

        @block.gpsimd
        def _(pool):
            pool.iota(g.place[:], pattern=[[P, TILES]], base=0, channel_multiplier=1,
                      allow_small_or_imprecise_dtypes=True).then_inc(done, 1)


def kernel(x, src, dst, edge_type_64, L1_gnn_edge_emb, L1_gnn_q_w, L1_gnn_k_w):
    import numpy as np
    import concourse.bacc as bacc
    from concourse.bass_utils import run_bass_kernel_spmd

    def tiled(a, pad):
        return np.pad(np.asarray(a), (0, ROWS - EDGES), constant_values=pad).reshape(P, TILES)

    arrays = {
        "in_x": np.ascontiguousarray(x), "in_src": tiled(src, NODES), "in_dst": tiled(dst, 0),
        "in_relation": tiled(edge_type_64, 0), "in_emb": np.ascontiguousarray(L1_gnn_edge_emb),
        "in_q_w": np.ascontiguousarray(L1_gnn_q_w), "in_k_w": np.ascontiguousarray(L1_gnn_k_w),
    }
    nc = bacc.Bacc("TRN2", target_bir_lowering=False, num_devices=1)
    args = [nc.dram_tensor(n, a.shape, mybir.dt.from_np(a.dtype), kind="ExternalInput").ap() for n, a in arrays.items()]
    out = nc.dram_tensor("out_0", (NODES, D), F32, kind="ExternalOutput").ap()
    build(nc, *args, out)
    return run_bass_kernel_spmd(nc, [arrays], core_ids=[0]).results[0]["out_0"]
```
